# Optimizing a Trainium2 kernel written in Bass

```python
import numpy as np
import jax
import jax.numpy as jnp

def _softmax(x, axis=-1):
    return jax.nn.softmax(x, axis=axis)

def _gelu(x):
    return jax.nn.gelu(x, approximate=True)

def _silu(x):
    return jax.nn.silu(x)

def _sigmoid(x):
    return jax.nn.sigmoid(x)

def _layernorm(x, axis=-1, eps=1e-05):
    m = jnp.mean(x, axis=axis, keepdims=True)
    v = jnp.var(x, axis=axis, keepdims=True)
    return (x - m) / jnp.sqrt(v + eps)

def _scatter_add(tgt, idx, src, axis=0):
    return tgt.at[idx].add(src)

def _segment_sum(src, seg, n):
    return jax.ops.segment_sum(src, seg, n)
kernel_name = 'mk_decoder_preln_d1_seqx_r2_5187ba'

def setup_inputs(seed: int=0):
    np.random.seed(seed)
    _w = jnp.asarray

    def _rec_inputs():
        import jax
        import jax.numpy as jnp
        _rk = jax.random.key(seed)
        x = 7.22e-05 + 1 * jax.random.normal(jax.random.fold_in(_rk, 1), (4, 1024, 512), jnp.float32)
        _lenS = 1024 - jax.random.randint(jax.random.fold_in(_rk, 7), (4,), 0, max(1, 1024 // 4) + 1, jnp.int32)
        _lenS2 = 1024 - jax.random.randint(jax.random.fold_in(_rk, 8), (4,), 0, max(1, 1024 // 4) + 1, jnp.int32)
        _ctx_1024P = jax.random.normal(jax.random.fold_in(_rk, 11), (4, 16, 512), jnp.float32)
        _ctx_1024c = jax.random.dirichlet(jax.random.fold_in(_rk, 511), 0.3 * jnp.ones((16,), jnp.float32), (4, 1024))
        _ctx_1024t = jnp.einsum('bsk,bkd->bsd', _ctx_1024c, _ctx_1024P)
        _ctx_1024t = _ctx_1024t * jax.lax.rsqrt(jnp.mean(jnp.square(_ctx_1024t)) + 1e-12) * 0.953939
        ctx_1024 = 4.13588e-05 + 0.999923 * (_ctx_1024t + 0.3 * jax.random.normal(jax.random.fold_in(_rk, 611), (4, 1024, 512), jnp.float32))
        _validS = jnp.arange(1024)[None, :] < _lenS[:, None]
        _validS2 = jnp.arange(1024)[None, :] < _lenS2[:, None]
        _causal = jnp.tril(jnp.ones((1024, 1024), dtype=bool))
        mask_BxS2_bf0 = jnp.logical_not(jnp.ones((4, 1024), dtype=bool))
        return (x, ctx_1024, mask_BxS2_bf0)
    x, ctx_1024, mask_BxS2_bf0 = _rec_inputs()

    def _L0_attn_setup():
        import jax, jax.numpy as jnp
        import numpy as np
        D_MODEL = 512
        D_STATE = 64
        D_CONV = 4
        EXPAND = 2
        HEADDIM = 64
        D_INNER = EXPAND * D_MODEL
        NHEADS = D_INNER // HEADDIM
        CONV_DIM = D_INNER + 2 * D_STATE
        D_IN_PROJ = 2 * D_INNER + 2 * D_STATE + NHEADS
        B, L = (2, 512)

        def _mamba2(x, in_proj_w, conv_w, conv_b, dt_bias, A_log, D_param, rms_w, out_proj_w):
            b, l, _ = x.shape
            zxbcdt = x @ in_proj_w.T
            z, xBC, dt = jnp.split(zxbcdt, [D_INNER, D_INNER + CONV_DIM], axis=-1)
            dt = jax.nn.softplus(dt + dt_bias)
            xBC = jax.lax.conv_general_dilated(xBC, conv_w, (1,), [(D_CONV - 1, 0)], dimension_numbers=('NLC', 'LIO', 'NLC'), feature_group_count=CONV_DIM) + conv_b
            xBC = jax.nn.silu(xBC)
            xs, Bmat, Cmat = jnp.split(xBC, [D_INNER, D_INNER + D_STATE], axis=-1)
            xh = xs.reshape(b, l, NHEADS, HEADDIM)
            A = -jnp.exp(A_log)
            dA = jnp.exp(dt * A)

            def step(h, inp):
                dA_t, dt_t, B_t, C_t, x_t = inp
                h = h * dA_t[..., None, None] + (dt_t[..., None] * x_t)[..., None] * B_t[:, None, None, :]
                y_t = jnp.einsum('bhpn,bn->bhp', h, C_t)
                return (h, y_t)
            h0 = jnp.zeros((b, NHEADS, HEADDIM, D_STATE), x.dtype)
            inps = (dA.transpose(1, 0, 2), dt.transpose(1, 0, 2), Bmat.transpose(1, 0, 2), Cmat.transpose(1, 0, 2), xh.transpose(1, 0, 2, 3))
            _, ys = jax.lax.scan(step, h0, inps)
            y = ys.transpose(1, 0, 2, 3) + D_param[None, None, :, None] * xh
            y = y.reshape(b, l, D_INNER)
            y = y * jax.nn.silu(z)
            y = y * jax.lax.rsqrt(jnp.mean(y * y, axis=-1, keepdims=True) + 1e-05) * rms_w
            return y @ out_proj_w.T
        key = jax.random.key(seed)
        ks = jax.random.split(key, 16)
        s = 0.02

        def mamba_params(i):
            kk = jax.random.split(ks[i], 8)
            dt = jnp.exp(jax.random.uniform(kk[4], (NHEADS,)) * (np.log(0.1) - np.log(0.001)) + np.log(0.001))
            dt_bias = dt + jnp.log(-jnp.expm1(-dt))
            return dict(in_proj_w=jax.random.normal(kk[0], (D_IN_PROJ, D_MODEL)) * s, conv_w=jax.random.normal(kk[1], (D_CONV, 1, CONV_DIM)) * 0.2, conv_b=jnp.zeros((CONV_DIM,)), dt_bias=dt_bias, A_log=jnp.log(jax.random.uniform(kk[2], (NHEADS,), minval=1.0, maxval=16.0)), D=jnp.ones((NHEADS,)), rms_w=jnp.ones((D_INNER,)), out_proj_w=jax.random.normal(kk[3], (D_MODEL, D_INNER)) * s)
        pf = mamba_params(1)
        pb = mamba_params(2)
        inp = {'x': jax.random.normal(ks[0], (B, L, D_MODEL))}
        for name, v in pf.items():
            inp['f_' + name] = v
        for name, v in pb.items():
            inp['b_' + name] = v
        inp['proj_w'] = jax.random.normal(ks[3], (D_MODEL, 2 * D_MODEL)) * s
        inp['proj_b'] = jnp.zeros((D_MODEL,))
        inp['ln_w'] = jnp.ones((D_MODEL,))
        inp['ln_b'] = jnp.zeros((D_MODEL,))
        return inp
    _L0_attn_all = _L0_attn_setup()
    _L0_attn_in = {k: v for k, v in _L0_attn_all.items() if k in ('f_in_proj_w', 'f_conv_w', 'f_conv_b', 'f_dt_bias', 'f_A_log', 'f_D', 'f_rms_w', 'f_out_proj_w', 'b_in_proj_w', 'b_conv_w', 'b_conv_b', 'b_dt_bias', 'b_A_log', 'b_D', 'b_rms_w', 'b_out_proj_w', 'proj_w', 'proj_b', 'ln_w', 'ln_b')}
    del _L0_attn_all

    def _L0_xattn_setup():
        import jax, jax.numpy as jnp
        import numpy as np
        import math
        B, S, D, H, NH = (4, 1024, 512, 512, 16)
        HD = H // NH
        key = jax.random.key(seed)
        ks = jax.random.split(key, 8)
        scale_in = math.sqrt(6.0 / (D + H))
        scale_out = math.sqrt(6.0 / (H + D))
        return {'q': jax.random.normal(ks[0], (B, S, D), jnp.float32), 'k': jax.random.normal(ks[1], (B, S, D), jnp.float32), 'v': jax.random.normal(ks[2], (B, S, D), jnp.float32), 'padding_mask': jnp.zeros((B, S), dtype=bool), 'W_q': jax.random.uniform(ks[3], (H, D), jnp.float32, -scale_in, scale_in), 'b_q': jnp.zeros((H,), jnp.float32), 'W_k': jax.random.uniform(ks[4], (H, D), jnp.float32, -scale_in, scale_in), 'b_k': jnp.zeros((H,), jnp.float32), 'W_v': jax.random.uniform(ks[5], (H, D), jnp.float32, -scale_in, scale_in), 'b_v': jnp.zeros((H,), jnp.float32), 'W_o': jax.random.uniform(ks[6], (D, H), jnp.float32, -scale_out, scale_out), 'b_o': jnp.zeros((D,), jnp.float32)}
    _L0_xattn_all = _L0_xattn_setup()
    _L0_xattn_in = {k: v for k, v in _L0_xattn_all.items() if k in ('W_q', 'b_q', 'W_k', 'b_k', 'W_v', 'b_v', 'W_o', 'b_o')}
    del _L0_xattn_all

    def _L0_ffn_setup():
        import jax, jax.numpy as jnp
        import numpy as np
        HIDDEN = 512
        HEAD_DIM = 64
        N_EXPERTS = 16
        MIN_EXPERTS = 2
        B, T = (4, 1024)

        def _normalize(x, axis):
            n = jnp.sqrt(jnp.sum(x * x, axis=axis, keepdims=True))
            return x / jnp.maximum(n, 1e-12)

        def _ste(x):
            hard = jax.lax.stop_gradient((x > 0).astype(x.dtype))
            return hard + x - jax.lax.stop_gradient(x)

        def _gating(hidden_states, sim_matrix, gates):
            b, t, c = hidden_states.shape
            flat = hidden_states.reshape(b * t, c)
            logits = _normalize(flat, -1) @ _normalize(sim_matrix, 0) - jax.nn.sigmoid(gates)
            gated = jax.nn.relu(logits)
            mask = _ste(gated)
            inactive = jnp.sum(mask, axis=1) == 0
            _, fb_idx = jax.lax.top_k(logits, MIN_EXPERTS)
            fb = jnp.zeros_like(mask).at[jnp.arange(b * t)[:, None], fb_idx].set(1.0)
            fb_applied = inactive[:, None] & (fb > 0)
            mask = jnp.where(fb_applied, 1.0, mask)
            masked_logits = jnp.where(mask > 0, gated, -jnp.inf)
            return jax.nn.softmax(masked_logits, axis=-1).reshape(b, t, -1)
        key = jax.random.key(seed)
        ks = jax.random.split(key, 6)
        xav_qkv = float(np.sqrt(6.0 / (HIDDEN + HEAD_DIM)))
        return {'hidden_states': jax.random.normal(ks[0], (B, T, HIDDEN), dtype=jnp.float32), 'sim_matrix': jax.random.normal(ks[1], (HIDDEN, N_EXPERTS), dtype=jnp.float32), 'gates': jnp.zeros((N_EXPERTS,), dtype=jnp.float32), 'q_proj': jax.random.uniform(ks[2], (N_EXPERTS, HIDDEN, HEAD_DIM), jnp.float32, -xav_qkv, xav_qkv), 'k_proj': jax.random.uniform(ks[3], (N_EXPERTS, HIDDEN, HEAD_DIM), jnp.float32, -xav_qkv, xav_qkv), 'v_proj': jax.random.uniform(ks[4], (N_EXPERTS, HIDDEN, HEAD_DIM), jnp.float32, -xav_qkv, xav_qkv), 'o_proj': jax.random.uniform(ks[5], (N_EXPERTS, HEAD_DIM, HIDDEN), jnp.float32, -xav_qkv, xav_qkv)}
    _L0_ffn_all = _L0_ffn_setup()
    _L0_ffn_in = {k: v for k, v in _L0_ffn_all.items() if k in ('sim_matrix', 'gates', 'q_proj', 'k_proj', 'v_proj', 'o_proj')}
    del _L0_ffn_all
    return {'x': x, 'ctx_1024': ctx_1024, 'mask_BxS2_bf0': mask_BxS2_bf0, 'L0_attn_f_in_proj_w': _L0_attn_in['f_in_proj_w'], 'L0_attn_f_conv_w': _L0_attn_in['f_conv_w'], 'L0_attn_f_conv_b': _L0_attn_in['f_conv_b'], 'L0_attn_f_dt_bias': _L0_attn_in['f_dt_bias'], 'L0_attn_f_A_log': _L0_attn_in['f_A_log'], 'L0_attn_f_D': _L0_attn_in['f_D'], 'L0_attn_f_rms_w': _L0_attn_in['f_rms_w'], 'L0_attn_f_out_proj_w': _L0_attn_in['f_out_proj_w'], 'L0_attn_b_in_proj_w': _L0_attn_in['b_in_proj_w'], 'L0_attn_b_conv_w': _L0_attn_in['b_conv_w'], 'L0_attn_b_conv_b': _L0_attn_in['b_conv_b'], 'L0_attn_b_dt_bias': _L0_attn_in['b_dt_bias'], 'L0_attn_b_A_log': _L0_attn_in['b_A_log'], 'L0_attn_b_D': _L0_attn_in['b_D'], 'L0_attn_b_rms_w': _L0_attn_in['b_rms_w'], 'L0_attn_b_out_proj_w': _L0_attn_in['b_out_proj_w'], 'L0_attn_proj_w': _L0_attn_in['proj_w'], 'L0_attn_proj_b': _L0_attn_in['proj_b'], 'L0_attn_ln_w': _L0_attn_in['ln_w'], 'L0_attn_ln_b': _L0_attn_in['ln_b'], 'L0_xattn_W_q': _L0_xattn_in['W_q'], 'L0_xattn_b_q': _L0_xattn_in['b_q'], 'L0_xattn_W_k': _L0_xattn_in['W_k'], 'L0_xattn_b_k': _L0_xattn_in['b_k'], 'L0_xattn_W_v': _L0_xattn_in['W_v'], 'L0_xattn_b_v': _L0_xattn_in['b_v'], 'L0_xattn_W_o': _L0_xattn_in['W_o'], 'L0_xattn_b_o': _L0_xattn_in['b_o'], 'L0_ffn_sim_matrix': _L0_ffn_in['sim_matrix'], 'L0_ffn_gates': _L0_ffn_in['gates'], 'L0_ffn_q_proj': _L0_ffn_in['q_proj'], 'L0_ffn_k_proj': _L0_ffn_in['k_proj'], 'L0_ffn_v_proj': _L0_ffn_in['v_proj'], 'L0_ffn_o_proj': _L0_ffn_in['o_proj']}

def reference(x, ctx_1024, mask_BxS2_bf0, L0_attn_f_in_proj_w, L0_attn_f_conv_w, L0_attn_f_conv_b, L0_attn_f_dt_bias, L0_attn_f_A_log, L0_attn_f_D, L0_attn_f_rms_w, L0_attn_f_out_proj_w, L0_attn_b_in_proj_w, L0_attn_b_conv_w, L0_attn_b_conv_b, L0_attn_b_dt_bias, L0_attn_b_A_log, L0_attn_b_D, L0_attn_b_rms_w, L0_attn_b_out_proj_w, L0_attn_proj_w, L0_attn_proj_b, L0_attn_ln_w, L0_attn_ln_b, L0_xattn_W_q, L0_xattn_b_q, L0_xattn_W_k, L0_xattn_b_k, L0_xattn_W_v, L0_xattn_b_v, L0_xattn_W_o, L0_xattn_b_o, L0_ffn_sim_matrix, L0_ffn_gates, L0_ffn_q_proj, L0_ffn_k_proj, L0_ffn_v_proj, L0_ffn_o_proj):
    import jax
    import jax.numpy as jnp

    def _L0_attn_ref(x, f_in_proj_w, f_conv_w, f_conv_b, f_dt_bias, f_A_log, f_D, f_rms_w, f_out_proj_w, b_in_proj_w, b_conv_w, b_conv_b, b_dt_bias, b_A_log, b_D, b_rms_w, b_out_proj_w, proj_w, proj_b, ln_w, ln_b):
        import jax, jax.numpy as jnp
        import numpy as np
        D_MODEL = 512
        D_STATE = 64
        D_CONV = 4
        EXPAND = 2
        HEADDIM = 64
        D_INNER = EXPAND * D_MODEL
        NHEADS = D_INNER // HEADDIM
        CONV_DIM = D_INNER + 2 * D_STATE
        D_IN_PROJ = 2 * D_INNER + 2 * D_STATE + NHEADS
        B, L = (2, 512)

        def _mamba2(x, in_proj_w, conv_w, conv_b, dt_bias, A_log, D_param, rms_w, out_proj_w):
            b, l, _ = x.shape
            zxbcdt = x @ in_proj_w.T
            z, xBC, dt = jnp.split(zxbcdt, [D_INNER, D_INNER + CONV_DIM], axis=-1)
            dt = jax.nn.softplus(dt + dt_bias)
            xBC = jax.lax.conv_general_dilated(xBC, conv_w, (1,), [(D_CONV - 1, 0)], dimension_numbers=('NLC', 'LIO', 'NLC'), feature_group_count=CONV_DIM) + conv_b
            xBC = jax.nn.silu(xBC)
            xs, Bmat, Cmat = jnp.split(xBC, [D_INNER, D_INNER + D_STATE], axis=-1)
            xh = xs.reshape(b, l, NHEADS, HEADDIM)
            A = -jnp.exp(A_log)
            dA = jnp.exp(dt * A)

            def step(h, inp):
                dA_t, dt_t, B_t, C_t, x_t = inp
                h = h * dA_t[..., None, None] + (dt_t[..., None] * x_t)[..., None] * B_t[:, None, None, :]
                y_t = jnp.einsum('bhpn,bn->bhp', h, C_t)
                return (h, y_t)
            h0 = jnp.zeros((b, NHEADS, HEADDIM, D_STATE), x.dtype)
            inps = (dA.transpose(1, 0, 2), dt.transpose(1, 0, 2), Bmat.transpose(1, 0, 2), Cmat.transpose(1, 0, 2), xh.transpose(1, 0, 2, 3))
            _, ys = jax.lax.scan(step, h0, inps)
            y = ys.transpose(1, 0, 2, 3) + D_param[None, None, :, None] * xh
            y = y.reshape(b, l, D_INNER)
            y = y * jax.nn.silu(z)
            y = y * jax.lax.rsqrt(jnp.mean(y * y, axis=-1, keepdims=True) + 1e-05) * rms_w
            return y @ out_proj_w.T
        out_fwd = _mamba2(x, f_in_proj_w, f_conv_w, f_conv_b, f_dt_bias, f_A_log, f_D, f_rms_w, f_out_proj_w)
        out_bwd = _mamba2(jnp.flip(x, 1), b_in_proj_w, b_conv_w, b_conv_b, b_dt_bias, b_A_log, b_D, b_rms_w, b_out_proj_w)
        out_bwd = jnp.flip(out_bwd, 1)
        combined = jnp.concatenate([out_fwd, out_bwd], axis=-1)
        h = x + combined @ proj_w.T + proj_b
        mu = jnp.mean(h, axis=-1, keepdims=True)
        var = jnp.mean((h - mu) ** 2, axis=-1, keepdims=True)
        return (h - mu) * jax.lax.rsqrt(var + 1e-05) * ln_w + ln_b

    def _L0_xattn_ref(q, k, v, padding_mask, W_q, b_q, W_k, b_k, W_v, b_v, W_o, b_o):
        import jax, jax.numpy as jnp
        import numpy as np
        import math
        B, S, D, H, NH = (4, 1024, 512, 512, 16)
        HD = H // NH
        b = q.shape[0]
        Q = (q @ W_q.T + b_q).reshape(b, -1, NH, HD).transpose(0, 2, 1, 3)
        K = (k @ W_k.T + b_k).reshape(b, -1, NH, HD).transpose(0, 2, 1, 3)
        V = (v @ W_v.T + b_v).reshape(b, -1, NH, HD).transpose(0, 2, 1, 3)
        scores = jnp.einsum('bhqd,bhkd->bhqk', Q, K) / math.sqrt(HD)
        sq = scores.shape[-2]
        causal = jnp.triu(jnp.ones((sq, sq), dtype=bool), k=1)
        scores = jnp.where(causal, -jnp.inf, scores)
        scores = jnp.where(padding_mask[:, None, None, :], -jnp.inf, scores)
        attn = jax.nn.softmax(scores, axis=-1)
        out = jnp.einsum('bhqk,bhkd->bhqd', attn, V)
        out = out.transpose(0, 2, 1, 3).reshape(b, -1, H)
        return out @ W_o.T + b_o

    def _L0_ffn_ref(hidden_states, sim_matrix, gates, q_proj, k_proj, v_proj, o_proj):
        import jax, jax.numpy as jnp
        import numpy as np
        HIDDEN = 512
        HEAD_DIM = 64
        N_EXPERTS = 16
        MIN_EXPERTS = 2
        B, T = (4, 1024)

        def _normalize(x, axis):
            n = jnp.sqrt(jnp.sum(x * x, axis=axis, keepdims=True))
            return x / jnp.maximum(n, 1e-12)

        def _ste(x):
            hard = jax.lax.stop_gradient((x > 0).astype(x.dtype))
            return hard + x - jax.lax.stop_gradient(x)

        def _gating(hidden_states, sim_matrix, gates):
            b, t, c = hidden_states.shape
            flat = hidden_states.reshape(b * t, c)
            logits = _normalize(flat, -1) @ _normalize(sim_matrix, 0) - jax.nn.sigmoid(gates)
            gated = jax.nn.relu(logits)
            mask = _ste(gated)
            inactive = jnp.sum(mask, axis=1) == 0
            _, fb_idx = jax.lax.top_k(logits, MIN_EXPERTS)
            fb = jnp.zeros_like(mask).at[jnp.arange(b * t)[:, None], fb_idx].set(1.0)
            fb_applied = inactive[:, None] & (fb > 0)
            mask = jnp.where(fb_applied, 1.0, mask)
            masked_logits = jnp.where(mask > 0, gated, -jnp.inf)
            return jax.nn.softmax(masked_logits, axis=-1).reshape(b, t, -1)
        b, t, c = hidden_states.shape
        rw = _gating(hidden_states, sim_matrix, gates)
        q = jnp.einsum('bte,bted->btd', rw, jnp.einsum('btc,ecd->bted', hidden_states, q_proj))
        k = jnp.einsum('bte,bted->btd', rw, jnp.einsum('btc,ecd->bted', hidden_states, k_proj))
        v = jnp.einsum('bte,bted->btd', rw, jnp.einsum('btc,ecd->bted', hidden_states, v_proj))
        scale = 1.0 / jnp.sqrt(jnp.asarray(HEAD_DIM, dtype=q.dtype))
        scores = jnp.einsum('bqd,bkd->bqk', q, k) * scale
        causal = jnp.tril(jnp.ones((t, t), dtype=bool))
        scores = jnp.where(causal, scores, -jnp.inf)
        attn = jnp.einsum('bqk,bkd->bqd', jax.nn.softmax(scores, axis=-1), v)
        mixed = attn[:, :, None, :] * rw[..., None]
        return jnp.einsum('bted,edc->btc', mixed, o_proj)
    x = x + _L0_attn_ref(_layernorm(x, axis=-1), L0_attn_f_in_proj_w, L0_attn_f_conv_w, L0_attn_f_conv_b, L0_attn_f_dt_bias, L0_attn_f_A_log, L0_attn_f_D, L0_attn_f_rms_w, L0_attn_f_out_proj_w, L0_attn_b_in_proj_w, L0_attn_b_conv_w, L0_attn_b_conv_b, L0_attn_b_dt_bias, L0_attn_b_A_log, L0_attn_b_D, L0_attn_b_rms_w, L0_attn_b_out_proj_w, L0_attn_proj_w, L0_attn_proj_b, L0_attn_ln_w, L0_attn_ln_b)
    x = x + _L0_xattn_ref(_layernorm(x, axis=-1), ctx_1024, ctx_1024, mask_BxS2_bf0, L0_xattn_W_q, L0_xattn_b_q, L0_xattn_W_k, L0_xattn_b_k, L0_xattn_W_v, L0_xattn_b_v, L0_xattn_W_o, L0_xattn_b_o)
    x = x + _L0_ffn_ref(_layernorm(x, axis=-1), L0_ffn_sim_matrix, L0_ffn_gates, L0_ffn_q_proj, L0_ffn_k_proj, L0_ffn_v_proj, L0_ffn_o_proj)
    return x

_drawn_inputs = setup_inputs


def setup_inputs(seed=0):
    import zlib

    import numpy as np

    out = dict(_drawn_inputs(seed))
    spreads = {'L0_attn_f_conv_b': (0.0, 0.1),
     'L0_attn_f_D': (1.0, 0.6),
     'L0_attn_f_rms_w': (1.0, 0.576),
     'L0_attn_b_conv_b': (0.0, 0.1),
     'L0_attn_b_D': (1.0, 0.6),
     'L0_attn_b_rms_w': (1.0, 0.578),
     'L0_attn_proj_b': (0.0, 0.1),
     'L0_attn_ln_w': (1.0, 0.2),
     'L0_attn_ln_b': (0.0, 0.1),
     'L0_xattn_b_q': (0.0, 0.755),
     'L0_xattn_b_k': (0.0, 0.8),
     'L0_xattn_b_v': (0.0, 0.1),
     'L0_xattn_b_o': (0.0, 0.1),
     'L0_ffn_gates': (0.0, 0.31)}
    factors = {'L0_attn_f_dt_bias': 8.0,
     'L0_attn_f_A_log': 8.0,
     'L0_attn_b_dt_bias': 8.0,
     'L0_attn_b_A_log': 8.0,
     'L0_ffn_q_proj': 4.794,
     'L0_ffn_k_proj': 4.823}
    for name, (base, spread) in spreads.items():
        noise = np.random.default_rng([zlib.crc32(name.encode()), seed]).standard_normal(out[name].shape)
        drawn = base * np.exp(spread * noise) if base else spread * noise
        out[name] = jnp.asarray(drawn.astype(out[name].dtype))
    for name, factor in factors.items():
        out[name] = (out[name] * factor).astype(out[name].dtype)
    return out
```

```python
from contextlib import ExitStack

import concourse.bass as bass
from concourse import mybir

F32 = mybir.dt.float32
F32R = mybir.dt.float32r
BF16 = mybir.dt.bfloat16
I32 = mybir.dt.int32
U8 = mybir.dt.uint8
ACT = mybir.ActivationFunctionType
ALU = mybir.AluOpType
AX = mybir.AxisListType

P = 128
B = 4
S = 1024
D = 512
KD = D // P
NT = S // P
BANK = 512
EPS = 1e-5
NEG = -1.0e30
RSQRT_SEED = float(0x5F3759DF)


class Signal:

    def __init__(self, held, nc, name, per, unit=1):
        self.sem = nc.alloc_semaphore(name)
        held.append(self.sem)
        self.per, self.unit = per, unit

    def start(self, eng):
        eng.sem_inc(self.sem, self.per * self.unit)

    def at(self, it, n):
        return it * (self.per * self.unit) + (self.per + n + 1) * self.unit


class Banks:

    def __init__(self, ctx, nc, name, n, uses, width=BANK):
        self.t = [ctx.enter_context(nc.psum_tensor(f"{name}{i}", [P, width], F32)) for i in range(n)]
        self.bank = {u[0]: i % n for i, u in enumerate(uses)}
        self.before = {}
        for b in range(n):
            mine = uses[b::n]
            for i, (key, _, _) in enumerate(mine):
                _, s, e = mine[i - 1]
                self.before[key] = (s, e if i else e - s.per)

    def __getitem__(self, key):
        return self.t[self.bank[key]]

    def open(self, pe, it, key):
        s, e = self.before[key]
        pe.wait_ge(s.sem, s.at(it, e))
        return self.t[self.bank[key]]


def matmul3(nc, out, w_hi, w_lo, x_hi, x_lo, first, last):
    nc.tensor.matmul(out, w_hi, x_hi, start=first, stop=False)
    nc.tensor.matmul(out, w_lo, x_hi, start=False, stop=False)
    return nc.tensor.matmul(out, w_hi, x_lo, start=False, stop=last)


def bcast(ap, axis, n):
    a = ap.unsqueeze(axis)
    shape = list(a.shape)
    shape[axis] = n
    return a.broadcast_to(shape)


class Chain:

    def __init__(self, sig, eng, it):
        self.sig, self.eng, self.it, self.n = sig, eng, it, 0

    def __call__(self, ins):
        ins.then_inc(self.sig.sem, 1)
        self.eng.wait_ge(self.sig.sem, self.sig.at(self.it, self.n))
        self.n += 1


RSQRT_STEPS = 11


def rsqrt(nc, step, out, x, v, a, scale, eps):
    step(nc.vector.tensor_scalar(v, x, scale, eps, ALU.mult, ALU.add))
    step(nc.vector.tensor_scalar(out.bitcast(I32), v.bitcast(I32), -0.5, RSQRT_SEED, ALU.mult, ALU.add))
    for _ in range(3):
        step(nc.vector.tensor_tensor(a, out, out, ALU.mult))
        step(nc.vector.scalar_tensor_tensor(a, a, -0.5, v, ALU.mult, ALU.mult))
        step(nc.vector.scalar_tensor_tensor(out, a, 1.5, out, ALU.add, ALU.mult))


def split_weight(nc, dve, stage, stage_loaded, hi_ready, half_ready, n, hi, lo):
    dve.wait_ge(stage_loaded, 16 * (n // 2 + 1))
    nc.vector.tensor_copy(hi, stage).then_inc(hi_ready, 1)
    dve.wait_ge(hi_ready, n + 1)
    nc.vector.tensor_tensor(lo, stage, hi.bitcast(F32), ALU.subtract).then_inc(half_ready, 1)


def identity(nc, pool, sem, tiles):
    for t in tiles[:-1]:
        nc.gpsimd.memset(t, 0.0)
    nc.gpsimd.memset(tiles[-1], 0.0).then_inc(sem, 1)
    pool.wait_ge(sem, 1)
    for t in tiles:
        last = nc.gpsimd.affine_select(t, t, [[-1, P]], ALU.not_equal, 1.0, base=0, channel_multiplier=1)
    last.then_inc(sem, 1)
    pool.wait_ge(sem, 2)


def release(nc, held):
    nc.all_engine_barrier()
    nc.clear_and_free_semaphores(held)
    nc.all_engine_barrier()


DI = 1024
NS = 64
NH = 16
HP = DI // NH
XBC = DI + 2 * NS
DIN = 2 * DI + 2 * NS + NH
TAPS = 4
MT = XBC // P
KI = DI // P
GT = 2
GN = GT * P
NG = NT // GT
HALO = TAPS - 1
MP = (MT + 1) // 2
ATANH = [1.0 / (2 * k + 1) for k in range(8)]
Q4 = 4
NQ = NH // Q4


def mamba_pass(nc, backward, x_in, w_in, conv_w, conv_b, dt_bias, a_log, d_skip, rms_w, w_out, w_proj,
               part, out=None, proj_b=None, ln_w=None, ln_b=None):
    tag = "mb_" if backward else "mf_"
    order_g = list(range(NG))[::-1] if backward else list(range(NG))
    order_t = list(range(GT))[::-1] if backward else list(range(GT))
    tile_of = [order_g[c // GT] * GT + order_t[c % GT] for c in range(NT)]
    data0 = 0 if backward else HALO
    halo0 = GN if backward else 0
    tail0 = 0 if backward else GN

    held = []
    with ExitStack() as ctx:
        def sb(name, shape, dt=F32):
            return ctx.enter_context(nc.sbuf_tensor(tag + name, shape, dt))

        def sig(name, per, unit=1):
            return Signal(held, nc, tag + name, per, unit)

        def sem(name):
            held.append(nc.alloc_semaphore(tag + name))
            return held[-1]

        w_hi, w_lo = sb("w_hi", [P, KD, DIN], F32R), sb("w_lo", [P, KD, DIN], F32R)
        wc = sb("wc", [P, KI, D])
        ident = sb("ident", [P, P])
        ident_b = sb("ident_b", [P, P], BF16)
        ones = sb("ones", [P, P])
        upto = sb("upto", [P, P])
        upto_r = sb("upto_r", [P, P], F32R)
        later = sb("later", [P, Q4, P], BF16)
        cw, cb = sb("cw", [P, MT, TAPS]), sb("cb", [P, MT])
        a_pos, dtb, dsk = sb("a_pos", [P, NH]), sb("dtb", [P, NH]), sb("dsk", [P, NH])
        rmsw = sb("rmsw", [P, KI])
        xg = sb("xg", [P, GT, D])
        stat, mv = sb("stat", [P, GT, 6]), sb("mv", [P, NT, 2])
        xr = sb("xr", [P, NT])
        gtmp = sb("gtmp", [P, 2, GT])
        xt_hi, xt_lo = sb("xt_hi", [P, 2, KD, GN], F32R), sb("xt_lo", [P, 2, KD, GN], F32R)
        xc = sb("xc", [P, MT, GN + HALO])
        cv = sb("cv", [P, MT, GN])
        xs = sb("xs", [P, 2, MT, GN])
        ct = sb("ct", [NS, 2, GN])
        u, au, ea, wa, wb, wd, wt, wr = [sb(n, [P, GT, NH]) for n in ("u", "au", "ea", "wa", "wb", "wd", "wt", "wr")]
        dt = sb("dt", [P, 2, GT, NH])
        ncs, ecs = sb("ncs", [P, 2, GT, NH]), sb("ecs", [P, 2, GT, NH])
        wend, etot = sb("wend", [P, 2, GT, NH]), sb("etot", [P, 2, GT, NH])
        da_hi, da_lo = sb("da_hi", [P, 2, GT, NH], F32R), sb("da_lo", [P, 2, GT, NH], F32R)
        gb = sb("gb", [P, P + NS])
        xtok, xdt, xw = sb("xtok", [P, DI]), sb("xdt", [P, DI]), sb("xw", [P, DI])
        decay = sb("decay", [P, 2, Q4, P])
        y = sb("y", [P, DI])
        zs = sb("zs", [P, 2, DI])
        yT = sb("yT", [P, KI, P])
        state = sb("state", [NS, DI])
        squares = sb("squares", [P, DI], BF16)
        ssq, ry, ytmp = sb("ssq", [P, 1]), sb("ry", [P, 1]), sb("ytmp", [P, 2])
        hb = sb("hb", [P, 2, D])
        if backward:
            partb, xres = sb("partb", [P, D]), sb("xres", [P, D])
            pjb, lnw, lnb = sb("pjb", [P, D]), sb("lnw", [P, D]), sb("lnb", [P, D])
            hstat, hmv, hr, htmp = sb("hstat", [P, 6]), sb("hmv", [P, 2]), sb("hr", [P, 1]), sb("htmp", [P, 2])
        stage = [cv[:].rearrange("p m n -> p (m n)")[:, 0:DIN], xc[:].rearrange("p m n -> p (m n)")[:, 0:DIN]]
        raw_out = xs[:].rearrange("p r m n -> p (r m n)")[:, 0:KD * DI].rearrange("p (k n) -> p k n", k=KD)
        raw_proj = xc[:].rearrange("p m n -> p (m n)")[:, 0:KD * D].rearrange("p (k n) -> p k n", k=KD)

        x_loaded = sig("x_loaded", NG, 16)
        xn_ready = sig("xn_ready", NG)
        xT_full = sig("xT_full", NT)
        xhi_ready = sig("xhi_ready", NT)
        xlo_ready = sig("xlo_ready", NT)
        dt_full = sig("dt_full", NG)
        au_ready = sig("au_ready", NG)
        ea_ready = sig("ea_ready", NG)
        da_ready = sig("da_ready", NG)
        cs_full = sig("cs_full", NG)
        sums_ready = sig("sums_ready", NG)
        dt_ready = sig("dt_ready", NG)
        m_full = sig("m_full", NG * MP)
        halo_ready = sig("halo_ready", NG)
        xc_ready = sig("xc_ready", NG * MP)
        tap_ready = sig("tap_ready", NG)
        conv_ready = sig("conv_ready", NG * TAPS)
        tanh_ready = sig("tanh_ready", NG)
        xs_ready = sig("xs_ready", NG)
        gb_full = sig("gb_full", NT)
        gb_ready = sig("gb_ready", NT)
        x_full = sig("x_full", NT * 2)
        xtok_ready = sig("xtok_ready", NT * 2)
        xdt_ready = sig("xdt_ready", NT)
        xw_ready = sig("xw_ready", NT)
        skip_ready = sig("skip_ready", NT)
        z_full = sig("z_full", NT * 2)
        zt_ready = sig("zt_ready", NT * 2)
        z_ready = sig("z_ready", NT * 2)
        d_full = sig("d_full", NT * NQ)
        exp_ready = sig("exp_ready", NT * NQ)
        mix_ready = sig("mix_ready", NT * NQ)
        intra_full = sig("intra_full", NT * NQ)
        inter_full = sig("inter_full", NT * 2)
        inter_ready = sig("inter_ready", NT * 2)
        base_ready = sig("base_ready", NT)
        sum_ready = sig("sum_ready", NT * 2)
        y_ready = sig("y_ready", NT)
        hdec_ready = sig("hdec_ready", NT)
        hnew_full = sig("hnew_full", NT * 2)
        state_ready = sig("state_ready", NT * 2 + 1)
        yT_full = sig("yT_full", NT * 2)
        yT_ready = sig("yT_ready", NT * 2)
        ssq_ready = sig("ssq_ready", NT)
        o_full = sig("o_full", NT)
        h_ready = sig("h_ready", NT)
        stored = [sig(f"stored{i}", NT // 2, 16) for i in range(2)]
        if backward:
            res_loaded = sig("res_loaded", NT * 2, 16)
            res_ready = sig("res_ready", NT)
            n_ready = sig("n_ready", NT)
            out_ready = sig("out_ready", NT)
            pool_step = sig("pool_step", NT * 3)
        else:
            out_ready = h_ready
        steps = NG * (2 + RSQRT_STEPS + 18) + NT * RSQRT_STEPS
        steps += NT * (2 + RSQRT_STEPS) if backward else 0
        dve_step = sig("dve_step", steps)
        passed_dve, passed_pool, passed_sp = sem("passed_dve"), sem("passed_pool"), sem("passed_sp")
        const_ready = sem("const_ready")
        par_loaded, par_ready = sem("par_loaded"), sem("par_ready")
        stage_loaded = [sem(f"stage_loaded{i}") for i in range(2)]
        raw_loaded = sem("raw_loaded")
        hi_ready, half_ready = sem("hi_ready"), sem("half_ready")
        wc_full = sem("wc_full")
        wc_ready = sem("wc_ready")

        def order():
            yield "group", 0
            for c in range(NT):
                yield "inputs", c
                if c % GT == 0 and c // GT + 1 < NG:
                    yield "group", c // GT + 1
                if c:
                    yield "output", c - 1
                yield "scan", c
            yield "output", NT - 1

        def run(steps):
            for what, n in order():
                if what in steps:
                    steps[what](n)

        proj, dec, yb, ib = [], [], [], []
        for what, n in order():
            if what == "group":
                proj += [(("xT", n, t), xlo_ready, n * GT + t) for t in range(GT)]
                proj += [(("dt", n), au_ready, n)]
                proj += [(("m", n, i), xc_ready, n * MP + i) for i in range(MP)]
                proj += [(("cs", n), sums_ready, n)]
            if what == "inputs":
                dec += [(("gb", n), gb_ready, n)]
                ib += [(("x", n, j), xtok_ready, 2 * n + j) for j in range(2)]
                proj += [(("z", n, j), z_ready, 2 * n + j) for j in range(2)]
            if what == "output":
                yb += [(("yT", n, j), yT_ready, 2 * n + j) for j in range(2)]
                ib += [(("o", n), h_ready, n)]
            if what == "scan":
                dec += [(("d", n, q), exp_ready, NQ * n + q) for q in range(NQ)]
                yb += [(("y", n, j), sum_ready, 2 * n + j) for j in range(2)]
                ib += [(("i", n, j), inter_ready, 2 * n + j) for j in range(2)]
                ib += [(("h", n, j), state_ready, 2 * n + j + 1) for j in range(2)]
        proj = Banks(ctx, nc, tag + "proj", 2, proj)
        dec = Banks(ctx, nc, tag + "dec", 2, dec)
        yb = Banks(ctx, nc, tag + "yb", 2, yb)
        ib = Banks(ctx, nc, tag + "ib", 2, ib)
        params = [(cw[:], conv_w), (cb[:], conv_b), (dtb[:], dt_bias), (a_pos[:], a_log), (dsk[:], d_skip), (rmsw[:], rms_w)]
        if backward:
            params += [(pjb[:], proj_b), (lnw[:], ln_w), (lnb[:], ln_b)]

        block = ctx.enter_context(nc.Block())

        @block.sync
        def _(sp):
            for s in [x_loaded] + stored + ([res_loaded] if backward else []):
                s.start(sp)
            for k in range(KD):
                if k >= 2:
                    sp.wait_ge(half_ready, k - 1)
                sp.dma_start(stage[k % 2], w_in[k * P:(k + 1) * P, :]).then_inc(stage_loaded[k % 2], 16)
                if k == 0:
                    for t, src in params:
                        sp.dma_start(t, src).then_inc(par_loaded, 16)
                    sp.dma_start(raw_out, w_out.rearrange("(k p) n -> p k n", p=P)).then_inc(raw_loaded, 16)
            sp.wait_ge(half_ready, KD)
            sp.dma_start(raw_proj, w_proj.rearrange("(k p) n -> p k n", p=P)).then_inc(raw_loaded, 16)
            sp.wait_ge(wc_ready, KI)
            with sp.Fori(0, B) as it:
                def group(g):
                    sp.wait_ge(xT_full.sem, xT_full.at(it, GT * g - 1))
                    sp.sem_inc(passed_sp, 1)
                    rows = slice(order_g[g] * GN, (order_g[g] + 1) * GN)
                    sp.dma_start(xg[:], x_in[it, rows, :].rearrange("(t p) d -> p t d", p=P)).then_inc(x_loaded.sem, 16)

                def output(c):
                    rows = slice(tile_of[c] * P, (tile_of[c] + 1) * P)
                    if backward:
                        sp.wait_ge(out_ready.sem, out_ready.at(it, c - 1))
                        sp.sem_inc(passed_sp, 1)
                        sp.dma_start(partb[:], part[it, rows, :]).then_inc(res_loaded.sem, 16)
                        sp.dma_start(xres[:], x_in[it, rows, :]).then_inc(res_loaded.sem, 16)
                    sp.wait_ge(out_ready.sem, out_ready.at(it, c))
                    sp.sem_inc(passed_sp, 1)
                    sp.dma_start((out if backward else part)[it, rows, :], hb[:, c % 2, :]).then_inc(stored[c % 2].sem, 16)

                run({"group": group, "output": output})
            for s in stored:
                sp.wait_ge(s.sem, (B + 1) * s.per * 16)

        @block.gpsimd
        def _(pool):
            for s in [tap_ready, xdt_ready, xw_ready, skip_ready, base_ready, y_ready, hdec_ready] + (
                    [res_ready, out_ready, pool_step] if backward else []):
                s.start(pool)
            g_ = nc.gpsimd
            g_.memset(later[:], 0.0)
            g_.memset(ones[:], 1.0)
            g_.memset(upto[:], 1.0)
            identity(nc, pool, const_ready, [ident[:], ident_b[:]])
            sign = -1 if backward else 1
            g_.affine_select(upto[:], upto[:], [[sign, P]], ALU.is_ge, 0.0, base=0, channel_multiplier=-sign)
            g_.affine_select(later[:], later[:], [[0, Q4], [sign, P]], ALU.is_ge, NEG, base=0, channel_multiplier=-sign)\
                .then_inc(const_ready, 1)
            pool.wait_ge(par_ready, 3)
            pool.wait_ge(wc_ready, KI)
            with pool.Fori(0, B) as it:
                step = Chain(pool_step, pool, it) if backward else None

                def group(g):
                    pool.wait_ge(xc_ready.sem, xc_ready.at(it, MP * g + MP - 1))
                    pool.wait_ge(xs_ready.sem, xs_ready.at(it, g - 1))
                    pool.sem_inc(passed_pool, 1)
                    for m in range(MT):
                        last = g_.tensor_scalar(cv[:, m, :], xc[:, m, data0:data0 + GN], cw[:, m, TAPS - 1:TAPS],
                                                cb[:, m:m + 1], ALU.mult, ALU.add)
                    last.then_inc(tap_ready.sem, 1)

                def heads(t):
                    return t.rearrange("p (h d) -> p h d", h=NH)

                def inputs(c):
                    g, t = c // GT, order_t[c % GT]
                    pool.wait_ge(dt_ready.sem, dt_ready.at(it, g))
                    pool.wait_ge(xtok_ready.sem, xtok_ready.at(it, 2 * c + 1))
                    pool.wait_ge(intra_full.sem, intra_full.at(it, NQ * c - 1))
                    g_.tensor_tensor(heads(xdt[:]), heads(xtok[:]), bcast(dt[:, g % 2, t, :], 2, HP), ALU.mult)\
                        .then_inc(xdt_ready.sem, 1)
                    pool.wait_ge(xdt_ready.sem, xdt_ready.at(it, c))
                    pool.wait_ge(hnew_full.sem, hnew_full.at(it, 2 * c - 1))
                    g_.tensor_tensor(heads(xw[:]), heads(xdt[:]), bcast(wend[:, g % 2, t, :], 2, HP), ALU.mult)\
                        .then_inc(xw_ready.sem, 1)
                    g_.tensor_tensor(heads(xtok[:]), heads(xtok[:]), bcast(dsk[:], 2, HP), ALU.mult)\
                        .then_inc(skip_ready.sem, 1)

                def scan(c):
                    g, t = c // GT, order_t[c % GT]
                    pool.wait_ge(inter_full.sem, inter_full.at(it, 2 * c + 1))
                    pool.wait_ge(state_ready.sem, state_ready.at(it, 2 * c))
                    g_.tensor_tensor(heads(state[:]), heads(state[:]), bcast(etot[0:NS, g % 2, t, :], 2, HP), ALU.mult)\
                        .then_inc(hdec_ready.sem, 1)
                    pool.wait_ge(skip_ready.sem, skip_ready.at(it, c))
                    pool.wait_ge(inter_ready.sem, inter_ready.at(it, 2 * c + 1))
                    g_.tensor_tensor(y[:], y[:], xtok[:], ALU.add).then_inc(base_ready.sem, 1)
                    pool.wait_ge(sum_ready.sem, sum_ready.at(it, 2 * c + 1))
                    pool.wait_ge(z_ready.sem, z_ready.at(it, 2 * c + 1))
                    g_.tensor_tensor(y[:], y[:], zs[:, c % 2, :], ALU.mult).then_inc(y_ready.sem, 1)

                def output(c):
                    h, tl = hb[:, c % 2, :], tile_of[c]
                    pool.wait_ge(res_loaded.sem, res_loaded.at(it, 2 * c + 1))
                    pool.wait_ge(stored[c % 2].sem, stored[c % 2].at(it, c // 2 - 1))
                    g_.tensor_tensor(partb[:], partb[:], pjb[:], ALU.add)
                    step(g_.tensor_scalar(h, xres[:], mv[:, tl, 0:1], xr[:, tl:tl + 1], ALU.subtract, ALU.mult))
                    g_.tensor_tensor(h, h, partb[:], ALU.add).then_inc(res_ready.sem, 1)
                    pool.wait_ge(n_ready.sem, n_ready.at(it, c))
                    step(g_.tensor_tensor(h, h, lnw[:], ALU.mult))
                    step(g_.tensor_tensor(h, h, lnb[:], ALU.add))
                    g_.tensor_tensor(h, h, xres[:], ALU.add).then_inc(out_ready.sem, 1)

                run({"group": group, "inputs": inputs, "scan": scan} | ({"output": output} if backward else {}))

        @block.scalar
        def _(act):
            for s in [xhi_ready, xc_ready, tanh_ready, ea_ready, dt_ready, gb_ready, xtok_ready, zt_ready,
                      exp_ready, ssq_ready, yT_ready]:
                s.start(act)
            a_ = nc.scalar
            act.wait_ge(par_loaded, 16 * len(params))
            a_.activation(a_pos[:], a_pos[:], ACT.Exp).then_inc(par_ready, 1)
            act.wait_ge(wc_ready, KI)
            with act.Fori(0, B) as it:
                def group(g):
                    r, cl = g % 2, (g - 1) * GT - 1
                    act.wait_ge(z_full.sem, z_full.at(it, 2 * cl + 1))
                    for t in range(GT):
                        act.wait_ge(xT_full.sem, xT_full.at(it, GT * g + t))
                        a_.activation(xt_hi[:, r, :, t * P:(t + 1) * P],
                                      proj["xT", g, t][:].rearrange("p (k n) -> p k n", k=KD), ACT.Copy)\
                            .then_inc(xhi_ready.sem, 1)
                    act.wait_ge(au_ready.sem, au_ready.at(it, g))
                    a_.activation(ea[:], au[:], ACT.Exp).then_inc(ea_ready.sem, 1)
                    act.wait_ge(halo_ready.sem, halo_ready.at(it, g))
                    for i in range(MP):
                        n = min(2, MT - 2 * i)
                        act.wait_ge(m_full.sem, m_full.at(it, MP * g + i))
                        a_.activation(xc[:, 2 * i:2 * i + n, data0:data0 + GN],
                                      proj["m", g, i][:, 0:n * GN].rearrange("p (m n) -> p m n", m=n), ACT.Copy)\
                            .then_inc(xc_ready.sem, 1)
                    act.wait_ge(sums_ready.sem, sums_ready.at(it, g))
                    a_.activation(ecs[:, r], wd[:], ACT.Exp)
                    a_.activation(wend[:, r], wt[:], ACT.Exp)
                    a_.activation(etot[:, r], wr[:], ACT.Exp).then_inc(dt_ready.sem, 1)
                    act.wait_ge(conv_ready.sem, conv_ready.at(it, TAPS * g + TAPS - 2))
                    act.wait_ge(x_full.sem, x_full.at(it, 2 * cl + 1))
                    a_.activation(xs[:, r], cv[:], ACT.Tanh).then_inc(tanh_ready.sem, 1)

                def inputs(c):
                    act.wait_ge(gb_full.sem, gb_full.at(it, c))
                    act.wait_ge(mix_ready.sem, mix_ready.at(it, NQ * c - 1))
                    act.wait_ge(hnew_full.sem, hnew_full.at(it, 2 * c - 1))
                    a_.activation(gb[:], dec["gb", c][:, 0:P + NS], ACT.Copy).then_inc(gb_ready.sem, 1)
                    act.wait_ge(base_ready.sem, base_ready.at(it, c - 1))
                    for j in range(2):
                        act.wait_ge(x_full.sem, x_full.at(it, 2 * c + j))
                        a_.activation(xtok[:, j * BANK:(j + 1) * BANK], ib["x", c, j][:], ACT.Copy)\
                            .then_inc(xtok_ready.sem, 1)
                    act.wait_ge(y_ready.sem, y_ready.at(it, c - 2))
                    for j in range(2):
                        act.wait_ge(z_full.sem, z_full.at(it, 2 * c + j))
                        a_.activation(zs[:, c % 2, j * BANK:(j + 1) * BANK], proj["z", c, j][:], ACT.Tanh)\
                            .then_inc(zt_ready.sem, 1)

                def scan(c):
                    g, t = c // GT, order_t[c % GT]
                    for q in range(NQ):
                        act.wait_ge(d_full.sem, d_full.at(it, NQ * c + q))
                        act.wait_ge(intra_full.sem, intra_full.at(it, NQ * c + q - 2))
                        for h in range(Q4):
                            n = Q4 * q + h
                            last = a_.activation(decay[:, q % 2, h, :], dec["d", c, q][:, h * P:(h + 1) * P], ACT.Exp,
                                                 bias=ncs[:, g % 2, t, n:n + 1])
                        last.then_inc(exp_ready.sem, 1)

                def output(c):
                    act.wait_ge(y_ready.sem, y_ready.at(it, c))
                    act.wait_ge(h_ready.sem, h_ready.at(it, c - 1))
                    a_.activation(squares[:], y[:], ACT.Square, accum_out=ssq[:]).then_inc(ssq_ready.sem, 1)
                    act.wait_ge(o_full.sem, o_full.at(it, c - 1))
                    for j in range(2):
                        act.wait_ge(yT_full.sem, yT_full.at(it, 2 * c + j))
                        a_.activation(yT[:, 4 * j:4 * j + 4, :], yb["yT", c, j][:].rearrange("p (k n) -> p k n", k=4),
                                      ACT.Copy).then_inc(yT_ready.sem, 1)

                run({"group": group, "inputs": inputs, "scan": scan, "output": output})

        @block.vector
        def _(dve):
            for s in [xn_ready, xlo_ready, au_ready, da_ready, sums_ready, halo_ready, conv_ready, xs_ready, z_ready,
                      mix_ready, inter_ready, sum_ready, state_ready, h_ready, dve_step] + ([n_ready] if backward else []):
                s.start(dve)
            v_ = nc.vector
            for k in range(KD):
                dve.wait_ge(stage_loaded[k % 2], 16 * (k // 2 + 1))
                for a, b, f in ((0, DI, 0.5), (DI, DIN, 1.0)):
                    src = stage[k % 2][:, a:b]
                    v_.tensor_scalar(w_hi[:, k, a:b], src, f, None, ALU.mult).then_inc(hi_ready, 1)
                    dve.wait_ge(hi_ready, 2 * k + 1 + int(a > 0))
                    last = v_.scalar_tensor_tensor(w_lo[:, k, a:b], src, f, w_hi[:, k, a:b].bitcast(F32), ALU.mult, ALU.subtract)
                last.then_inc(half_ready, 1)
            dve.wait_ge(par_loaded, 16 * len(params))
            v_.tensor_scalar(cw[:], cw[:], 0.5, None, ALU.mult).then_inc(par_ready, 1)
            v_.tensor_scalar(cb[:], cb[:], 0.5, None, ALU.mult).then_inc(par_ready, 1)
            dve.wait_ge(const_ready, 3)
            v_.tensor_copy(upto_r[:], upto[:])
            for i in range(KI):
                dve.wait_ge(wc_full, i + 1)
                v_.tensor_scalar(wc[:, i, :], yb.t[i % 2][:], rmsw[:, i:i + 1], None, ALU.mult).then_inc(wc_ready, 1)
            dve.wait_ge(par_ready, 3)
            with dve.Fori(0, B) as it:
                step = Chain(dve_step, dve, it)
                dve.wait_ge(state_ready.sem, state_ready.at(it, -1))
                v_.memset(state[:], 0.0).then_inc(state_ready.sem, 1)

                def group(g):
                    r, cl = g % 2, (g - 1) * GT - 1
                    tg = order_g[g]
                    tiles = slice(tg * GT, (tg + 1) * GT)
                    dve.wait_ge(x_loaded.sem, x_loaded.at(it, g))
                    if backward:
                        dve.wait_ge(out_ready.sem, out_ready.at(it, GT * (g + 1) - 1 - NT))
                    for t in range(GT):
                        last = v_.bn_stats(stat[:, t, :], xg[:, t, :])
                    step(last)
                    dve.sem_inc(passed_dve, 1)
                    for t in range(GT):
                        last = v_.bn_aggr(mv[:, tg * GT + t, :], stat[:, t, :])
                    step(last)
                    rsqrt(nc, step, xr[:, tiles], mv[:, tiles, 1], gtmp[:, 0, :], gtmp[:, 1, :], 1.0, EPS)
                    for t in range(GT):
                        n = tg * GT + t
                        last = v_.tensor_scalar(xg[:, t, :], xg[:, t, :], mv[:, n, 0:1], xr[:, n:n + 1], ALU.subtract, ALU.mult)
                    last.then_inc(xn_ready.sem, 1)
                    dve.wait_ge(z_full.sem, z_full.at(it, 2 * cl + 1))
                    for t in range(GT):
                        dve.wait_ge(xhi_ready.sem, xhi_ready.at(it, GT * g + t))
                        sl = slice(t * P, (t + 1) * P)
                        v_.tensor_tensor(xt_lo[:, r, :, sl], proj["xT", g, t][:].rearrange("p (k n) -> p k n", k=KD),
                                         xt_hi[:, r, :, sl].bitcast(F32), ALU.subtract).then_inc(xlo_ready.sem, 1)
                    dve.wait_ge(conv_ready.sem, conv_ready.at(it, TAPS * g - 1))
                    halo = xc[:, :, halo0:halo0 + HALO]
                    if g == 0:
                        v_.memset(halo, 0.0).then_inc(halo_ready.sem, 1)
                    else:
                        v_.tensor_copy(halo, xc[:, :, tail0:tail0 + HALO]).then_inc(halo_ready.sem, 1)
                    dve.wait_ge(dt_ready.sem, dt_ready.at(it, g - 1))
                    dve.wait_ge(dt_full.sem, dt_full.at(it, g))
                    step(v_.tensor_tensor(u[:], proj["dt", g][:, 0:GT * NH].rearrange("p (t h) -> p t h", t=GT),
                                          bcast(dtb[:], 1, GT), ALU.add))
                    v_.scalar_tensor_tensor(au[:], u[:], -1.0, u[:], ALU.mult, ALU.min).then_inc(au_ready.sem, 1)
                    dve.wait_ge(ea_ready.sem, ea_ready.at(it, g))
                    step(v_.tensor_scalar(wa[:], ea[:], 2.0, None, ALU.add))
                    step(v_.reciprocal(wb[:], wa[:]))
                    step(v_.tensor_tensor(wd[:], ea[:], wb[:], ALU.mult))
                    step(v_.tensor_tensor(wa[:], wd[:], wd[:], ALU.mult))
                    step(v_.tensor_scalar(wb[:], wa[:], ATANH[-1], None, ALU.mult))
                    for k in range(len(ATANH) - 2, 0, -1):
                        step(v_.scalar_tensor_tensor(wb[:], wb[:], ATANH[k], wa[:], ALU.add, ALU.mult))
                    step(v_.scalar_tensor_tensor(wb[:], wb[:], 1.0, wd[:], ALU.add, ALU.mult))
                    step(v_.tensor_scalar(wt[:], u[:], 0.0, None, ALU.max))
                    dve.wait_ge(hdec_ready.sem, hdec_ready.at(it, cl))
                    dve.wait_ge(exp_ready.sem, exp_ready.at(it, NQ * cl + 3))
                    dve.wait_ge(d_full.sem, d_full.at(it, NQ * cl + 3))
                    step(v_.scalar_tensor_tensor(dt[:, r], wb[:], 2.0, wt[:], ALU.mult, ALU.add))
                    step(v_.scalar_tensor_tensor(wr[:], dt[:, r], -1.0, bcast(a_pos[:], 1, GT), ALU.mult, ALU.mult))
                    step(v_.tensor_copy(da_hi[:, r], wr[:]))
                    v_.tensor_tensor(da_lo[:, r], wr[:], da_hi[:, r].bitcast(F32), ALU.subtract).then_inc(da_ready.sem, 1)
                    dve.wait_ge(tap_ready.sem, tap_ready.at(it, g))
                    for i, j in enumerate(range(TAPS - 2, -1, -1)):
                        a = TAPS - 1 - j if backward else j
                        for m in range(MT):
                            last = v_.scalar_tensor_tensor(cv[:, m, :], xc[:, m, a:a + GN], cw[:, m, j:j + 1], cv[:, m, :],
                                                           ALU.mult, ALU.add)
                        last.then_inc(conv_ready.sem, 1)
                        dve.wait_ge(conv_ready.sem, conv_ready.at(it, TAPS * g + i))
                    dve.wait_ge(cs_full.sem, cs_full.at(it, g))
                    cs = proj["cs", g][:, 0:GT * NH].rearrange("p (t h) -> p t h", t=GT)
                    tot = proj["cs", g][:, GT * NH:2 * GT * NH].rearrange("p (t h) -> p t h", t=GT)
                    step(v_.tensor_scalar(ncs[:, r], cs, -1.0, None, ALU.mult))
                    v_.tensor_copy(wd[:], cs)
                    v_.tensor_tensor(wt[:], tot, ncs[:, r], ALU.add)
                    v_.tensor_copy(wr[:], tot).then_inc(sums_ready.sem, 1)
                    dve.wait_ge(tanh_ready.sem, tanh_ready.at(it, g))
                    dve.wait_ge(inter_full.sem, inter_full.at(it, 2 * cl + 1))
                    v_.scalar_tensor_tensor(ct[:, r, :], xs[NS:P, r, MT - 1, :], 1.0, cv[NS:P, MT - 1, :], ALU.add, ALU.mult)\
                        .then_inc(conv_ready.sem, 1)
                    dve.wait_ge(conv_ready.sem, conv_ready.at(it, TAPS * g + TAPS - 1))
                    v_.scalar_tensor_tensor(xs[:, r], xs[:, r], 1.0, cv[:], ALU.add, ALU.mult).then_inc(xs_ready.sem, 1)

                def inputs(c):
                    for j in range(2):
                        dve.wait_ge(zt_ready.sem, zt_ready.at(it, 2 * c + j))
                        z = zs[:, c % 2, j * BANK:(j + 1) * BANK]
                        v_.scalar_tensor_tensor(z, z, 1.0, proj["z", c, j][:], ALU.add, ALU.mult).then_inc(z_ready.sem, 1)

                def scan(c):
                    g, t = c // GT, order_t[c % GT]

                    def half(a, j):
                        return a[:, j * BANK:(j + 1) * BANK]

                    dve.wait_ge(gb_ready.sem, gb_ready.at(it, c))
                    for q in range(NQ):
                        dve.wait_ge(exp_ready.sem, exp_ready.at(it, NQ * c + q))
                        v_.tensor_tensor(decay[:, q % 2], decay[:, q % 2], bcast(gb[:, 0:P], 1, Q4), ALU.mult)\
                            .then_inc(mix_ready.sem, 1)
                    dve.wait_ge(yT_full.sem, yT_full.at(it, 2 * c - 1))
                    dve.wait_ge(ssq_ready.sem, ssq_ready.at(it, c - 1))
                    for j in range(2):
                        dve.wait_ge(inter_full.sem, inter_full.at(it, 2 * c + j))
                        v_.tensor_tensor(half(y, j).rearrange("p (h d) -> p h d", d=HP),
                                         ib["i", c, j][:].rearrange("p (h d) -> p h d", d=HP),
                                         bcast(ecs[:, g % 2, t, 8 * j:8 * j + 8], 2, HP), ALU.mult).then_inc(inter_ready.sem, 1)
                    dve.wait_ge(hdec_ready.sem, hdec_ready.at(it, c))
                    for j in range(2):
                        dve.wait_ge(hnew_full.sem, hnew_full.at(it, 2 * c + j))
                        v_.tensor_tensor(half(state, j), ib["h", c, j][0:NS, :], half(state, j), ALU.add)\
                            .then_inc(state_ready.sem, 1)
                    dve.wait_ge(base_ready.sem, base_ready.at(it, c))
                    for j in range(2):
                        dve.wait_ge(intra_full.sem, intra_full.at(it, NQ * c + 2 * j + 1))
                        v_.tensor_tensor(half(y, j), yb["y", c, j][:], half(y, j), ALU.add).then_inc(sum_ready.sem, 1)

                def output(c):
                    h = hb[:, c % 2, :]
                    dve.wait_ge(ssq_ready.sem, ssq_ready.at(it, c))
                    rsqrt(nc, step, ry[:], ssq[:], ytmp[:, 0:1], ytmp[:, 1:2], 1.0 / DI, EPS)
                    dve.wait_ge(o_full.sem, o_full.at(it, c))
                    if not backward:
                        dve.wait_ge(stored[c % 2].sem, stored[c % 2].at(it, c // 2 - 1))
                        v_.tensor_scalar(h, ib["o", c][:], ry[:, 0:1], None, ALU.mult).then_inc(h_ready.sem, 1)
                        return
                    dve.wait_ge(res_ready.sem, res_ready.at(it, c))
                    v_.scalar_tensor_tensor(h, ib["o", c][:], ry[:, 0:1], h, ALU.mult, ALU.add).then_inc(h_ready.sem, 1)
                    dve.wait_ge(h_ready.sem, h_ready.at(it, c))
                    step(v_.bn_stats(hstat[:], h))
                    dve.sem_inc(passed_dve, 1)
                    step(v_.bn_aggr(hmv[:], hstat[:]))
                    rsqrt(nc, step, hr[:], hmv[:, 1:2], htmp[:, 0:1], htmp[:, 1:2], 1.0, EPS)
                    v_.tensor_scalar(h, h, hmv[:, 0:1], hr[:, 0:1], ALU.subtract, ALU.mult).then_inc(n_ready.sem, 1)

                run({"group": group, "inputs": inputs, "scan": scan, "output": output})
                assert step.n == steps, (step.n, steps)

        @block.tensor
        def _(pe):
            for s in [xT_full, dt_full, cs_full, m_full, gb_full, x_full, z_full, d_full, intra_full, inter_full,
                      hnew_full, yT_full, o_full]:
                s.start(pe)
            mm, tr = nc.tensor.matmul, nc.tensor.transpose
            pe.wait_ge(raw_loaded, 32)
            for i in range(KI):
                if i >= 2:
                    pe.wait_ge(wc_ready, i - 1)
                for k in range(KD):
                    last = mm(yb.t[i % 2][:], raw_out[:, k, i * P:(i + 1) * P], raw_proj[:, k, :], start=k == 0, stop=k == KD - 1)
                last.then_inc(wc_full, 1)
            pe.wait_ge(const_ready, 3)
            with pe.Fori(0, B) as it:
                def group(g):
                    r = g % 2
                    pe.wait_ge(xn_ready.sem, xn_ready.at(it, g))
                    for t in range(GT):
                        ps = proj.open(pe, it, ("xT", g, t))
                        for k in range(KD):
                            last = tr(ps[:, k * P:(k + 1) * P], xg[:, t, k * P:(k + 1) * P], ident[:])
                        last.then_inc(xT_full.sem, 1)
                    pe.wait_ge(xlo_ready.sem, xlo_ready.at(it, GT * g + GT - 1))
                    ps = proj.open(pe, it, ("dt", g))
                    for t in range(GT):
                        for k in range(KD):
                            sl, cols = slice(t * P, (t + 1) * P), slice(DIN - NH, DIN)
                            last = matmul3(nc, ps[:, t * NH:(t + 1) * NH], xt_hi[:, r, k, sl], xt_lo[:, r, k, sl],
                                           w_hi[:, k, cols], w_lo[:, k, cols], k == 0, k == KD - 1)
                    last.then_inc(dt_full.sem, 1)
                    for i in range(MP):
                        ps = proj.open(pe, it, ("m", g, i))
                        for m in range(2 * i, min(2 * i + 2, MT)):
                            for k in range(KD):
                                cols = slice(DI + m * P, DI + (m + 1) * P)
                                last = matmul3(nc, ps[:, (m % 2) * GN:(m % 2 + 1) * GN], w_hi[:, k, cols], w_lo[:, k, cols],
                                               xt_hi[:, r, k, :], xt_lo[:, r, k, :], k == 0, k == KD - 1)
                        last.then_inc(m_full.sem, 1)
                    pe.wait_ge(da_ready.sem, da_ready.at(it, g))
                    ps = proj.open(pe, it, ("cs", g))
                    n = GT * NH
                    mm(ps[:, 0:n], upto[:], wr[:].rearrange("p t h -> p (t h)"), start=True, stop=True)
                    mm(ps[:, n:2 * n], ones[:], wr[:].rearrange("p t h -> p (t h)"), start=True, stop=True).then_inc(cs_full.sem, 1)

                def inputs(c):
                    g, r, t = c // GT, c // GT % 2, order_t[c % GT]
                    sl = slice(t * P, (t + 1) * P)
                    pe.wait_ge(xs_ready.sem, xs_ready.at(it, g))
                    ps = dec.open(pe, it, ("gb", c))
                    mm(ps[:, 0:P], xs[0:NS, r, MT - 1, sl], ct[:, r, sl], start=True, stop=True)
                    tr(ps[:, P:P + NS], xs[0:NS, r, MT - 1, sl], ident[0:NS, 0:NS]).then_inc(gb_full.sem, 1)
                    for j in range(2):
                        ps = ib.open(pe, it, ("x", c, j))
                        for k in range(4):
                            last = tr(ps[:, k * P:(k + 1) * P], xs[:, r, 4 * j + k, sl], ident[:])
                        last.then_inc(x_full.sem, 1)
                    for j in range(2):
                        ps = proj.open(pe, it, ("z", c, j))
                        for k in range(KD):
                            cols = slice(j * BANK, (j + 1) * BANK)
                            last = matmul3(nc, ps[:], xt_hi[:, r, k, sl], xt_lo[:, r, k, sl],
                                           w_hi[:, k, cols], w_lo[:, k, cols], k == 0, k == KD - 1)
                        last.then_inc(z_full.sem, 1)

                def scan(c):
                    g, r, t = c // GT, c // GT % 2, order_t[c % GT]
                    sl = slice(t * P, (t + 1) * P)

                    def intra(q):
                        ps = yb.open(pe, it, ("y", c, q // 2)) if q % 2 == 0 else yb["y", c, q // 2]
                        pe.wait_ge(mix_ready.sem, mix_ready.at(it, NQ * c + q))
                        for h in range(Q4):
                            n = Q4 * q + h
                            last = mm(ps[:, n % 8 * HP:(n % 8 + 1) * HP], decay[:, q % 2, h, :], xdt[:, n * HP:(n + 1) * HP],
                                      start=True, stop=True)
                        last.then_inc(intra_full.sem, 1)

                    for q in range(NQ):
                        ps = dec.open(pe, it, ("d", c, q))
                        mm(ps[:], ident_b[:], later[:].rearrange("p q n -> p (q n)"), start=True, stop=False)
                        for h in range(Q4):
                            n = Q4 * q + h
                            for half in (da_hi, da_lo):
                                last = mm(ps[:, h * P:(h + 1) * P], half[:, r, t, n:n + 1].broadcast_to([P, P]), upto_r[:],
                                          start=False,
                                          stop=half is da_lo and h == Q4 - 1)
                        last.then_inc(d_full.sem, 1)
                        if q == 0:
                            pe.wait_ge(xdt_ready.sem, xdt_ready.at(it, c))
                        else:
                            intra(q - 1)
                    pe.wait_ge(state_ready.sem, state_ready.at(it, 2 * c))
                    for j in range(2):
                        ps = ib.open(pe, it, ("i", c, j))
                        mm(ps[:], ct[:, r, sl], state[:, j * BANK:(j + 1) * BANK], start=True, stop=True)\
                            .then_inc(inter_full.sem, 1)
                    intra(NQ - 1)
                    pe.wait_ge(xw_ready.sem, xw_ready.at(it, c))
                    for j in range(2):
                        ps = ib.open(pe, it, ("h", c, j))
                        mm(ps[0:NS, :], gb[:, P:P + NS], xw[:, j * BANK:(j + 1) * BANK], start=True, stop=True)\
                            .then_inc(hnew_full.sem, 1)

                def output(c):
                    pe.wait_ge(y_ready.sem, y_ready.at(it, c))
                    for j in range(2):
                        ps = yb.open(pe, it, ("yT", c, j))
                        for k in range(4):
                            last = tr(ps[:, k * P:(k + 1) * P], y[:, (4 * j + k) * P:(4 * j + k + 1) * P], ident[:])
                        last.then_inc(yT_full.sem, 1)
                    pe.wait_ge(yT_ready.sem, yT_ready.at(it, 2 * c + 1))
                    ps = ib.open(pe, it, ("o", c))
                    for k in range(KI):
                        last = mm(ps[:], yT[:, k, :], wc[:, k, :], start=k == 0, stop=k == KI - 1)
                    last.then_inc(o_full.sem, 1)

                run({"group": group, "inputs": inputs, "scan": scan, "output": output})
    release(nc, held)


XH = 16
XD = D // XH
HG = P // XD
NHG = XH // HG
XSCALE = XD ** -0.5
ROW_MASK, ROW_MAX = 3 * XD, 3 * XD + 1
SLOTS = 3
VW = XD + 1


def pieces():
    out = []
    for j in range(NT):
        a = j * P
        while a < S:
            n = min(BANK, S - a)
            out.append((j, a, n))
            a += n
    return out


def cross_attention(nc, x_in, ctx_in, mask_in, wts, bq, bk, bv, bo, out):
    tag = "xa_"
    PC = pieces()
    NP = len(PC)
    held = []
    with ExitStack() as ctx:
        def sb(name, shape, dt=F32):
            return ctx.enter_context(nc.sbuf_tensor(tag + name, shape, dt))

        def sig(name, per, unit=1):
            return Signal(held, nc, tag + name, per, unit)

        def sem(name):
            held.append(nc.alloc_semaphore(tag + name))
            return held[-1]

        w_hi = [sb(f"w{n}_hi", [P, KD, D], F32R) for n in "qkv"]
        w_lo = [sb(f"w{n}_lo", [P, KD, D], F32R) for n in "qkv"]
        wo = sb("wo", [P, KD, D])
        ident, ident_b = sb("ident", [P, P]), sb("ident_b", [P, P], BF16)
        later_k, later_q = sb("later_k", [P, P], BF16), sb("later_q", [P, P], BF16)
        bqc, bkc = sb("bqc", [P, KD]), sb("bkc", [P, KD])
        bvr, bor = sb("bvr", [P, D]), sb("bor", [P, D])
        src = sb("src", [P, 2, D])
        stat, mv, xr, tmp = sb("stat", [P, 6]), sb("mv", [P, 2]), sb("xr", [P, 1]), sb("tmp", [P, 2])
        st_hi, st_lo = sb("st_hi", [P, KD, S], F32R), sb("st_lo", [P, KD, S], F32R)
        k_hi, k_lo = sb("k_hi", [P, NHG, S], F32R), sb("k_lo", [P, NHG, S], F32R)
        q_hi, q_lo = sb("q_hi", [P, S], F32R), sb("q_lo", [P, S], F32R)
        qa = [sb(f"qa{i}", [P, S], F32R) for i in range(SLOTS)]
        ka = [sb(f"ka{i}", [P, S], F32R) for i in range(SLOTS)]
        mask8 = sb("mask8", [P, S], U8)
        vv = sb("vv", [P, NT, XH, VW])
        pe_x = sb("pexp", [P, 4, BANK])
        mx, mrow = sb("mx", [P, 2, NT]), sb("mrow", [P, 2, NT, 2])
        rc = sb("rc", [P, NT])
        oo = sb("oo", [P, NT, D])
        oT = sb("oT", [P, KD, P])
        res = src
        stage = [oo[:].rearrange("p t d -> p (t d)")[:, i * KD * D:(i + 1) * KD * D].rearrange("p (k n) -> p k n", k=KD)
                 for i in range(2)]

        def slot(h):
            return h % SLOTS if h < XH - 1 or XH % SLOTS != 1 else 0

        used = [[h for h in range(XH) if slot(h) == s] for s in range(SLOTS)]

        def before(h):
            u = used[slot(h)]
            i = u.index(h)
            return u[i - 1] - (0 if i else XH)

        src_loaded = [sig(f"src_loaded{i}", NT, 16) for i in range(2)]
        mask_loaded = sig("mask_loaded", 1, 16)
        mask_ready = sig("mask_ready", 1)
        xn_ready = sig("xn_ready", NT)
        srcT_full = sig("srcT_full", 2 * NT)
        shi_ready = sig("shi_ready", 2 * NT)
        slo_ready = sig("slo_ready", 2 * NT)
        k_full = sig("k_full", 2 * NHG)
        khi_ready = sig("khi_ready", 2 * NHG)
        klo_ready = sig("klo_ready", 2 * NHG)
        v_full = sig("v_full", NT)
        v_ready = sig("v_ready", NT)
        q_full = sig("q_full", 2 * NHG)
        qhi_ready = sig("qhi_ready", 2 * NHG)
        qlo_ready = sig("qlo_ready", 2 * NHG)
        rows_loaded = [sig(f"rows_loaded{i}", 6 * len(used[i]), 16) for i in range(SLOTS)]
        s1_full = sig("s1_full", XH * NT)
        mx_ready = sig("mx_ready", XH * NT)
        nm_ready = sig("nm_ready", XH)
        mT_full = sig("mT_full", XH * 2)
        mrow_ready = sig("mrow_ready", XH * 2)
        s2_full = sig("s2_full", XH * NP)
        p_ready = sig("p_ready", XH * NP)
        av_full = sig("av_full", XH * NP)
        rc_ready = sig("rc_ready", XH)
        head_ready = sig("head_ready", XH)
        oT_full = sig("oT_full", NT)
        oT_ready = sig("oT_ready", NT)
        o_full = sig("o_full", NT)
        res_loaded = [sig(f"res_loaded{i}", NT // 2, 16) for i in range(2)]
        resb_ready = sig("resb_ready", NT)
        out_ready = sig("out_ready", NT)
        stored = [sig(f"stored{i}", NT // 2, 16) for i in range(2)]
        dve_step = sig("dve_step", NT * (2 + RSQRT_STEPS))
        const_ready, par_loaded, const_dve = sem("const_ready"), sem("par_loaded"), sem("const_dve")
        stage_loaded = [sem(f"stage_loaded{i}") for i in range(2)]
        hi_ready, half_ready = sem("hi_ready"), sem("half_ready")
        passed_sp, passed_dve = sem("passed_sp"), sem("passed_dve")

        def order():
            for n in range(NT):
                yield "src", n
            yield "mask", 0
            for i in range(2 * NHG):
                yield "k", i
            for t in range(NT):
                yield "v", t
            for n in range(NT, 2 * NT):
                yield "src", n
            for i in range(2):
                yield "q", i
            for h in range(SLOTS):
                yield "load", h
            for i in range(NT):
                yield "p1", (0, i)
            yield "nm", 0
            for h in range(XH):
                for s in range(NP):
                    yield "p2", (h, s)
                    if s < NT and h + 1 < XH:
                        yield "p1", (h + 1, s)
                    if s == NT and h + 1 < XH:
                        yield "nm", h + 1
                    if s >= 2:
                        yield "av", (h, s - 2)
                yield "av", (h, NP - 2)
                yield "av", (h, NP - 1)
                yield "head", h
                if h % HG == 1 and h // HG + 1 < NHG:
                    for i in range(2):
                        yield "q", 2 * (h // HG + 1) + i
                if h + SLOTS < XH:
                    yield "load", h + SLOTS
            for t in range(NT):
                yield "o", t

        def run(steps):
            for what, n in order():
                if what in steps:
                    steps[what](*n) if isinstance(n, tuple) else steps[what](n)

        gen, s1, acc = [], [], []
        for what, n in order():
            if what == "src":
                gen += [(("src", n), slo_ready, n)]
            if what in "kq":
                gen += [((what, n), klo_ready if what == "k" else qlo_ready, n)]
            if what == "v":
                gen += [((what, n), v_ready, n)]
            if what == "nm":
                gen += [(("mT", n, j), mrow_ready, 2 * n + j) for j in range(2)]
            if what == "p1":
                s1 += [(n, mx_ready, n[0] * NT + n[1])]
            if what == "p2":
                gen += [(("p2", *n), p_ready, n[0] * NP + n[1])]
            if what == "head":
                acc += [(n, head_ready, n)]
            if what == "o":
                gen += [(("oT", n), oT_ready, n), (("o", n), out_ready, n)]
        gen = Banks(ctx, nc, tag + "gen", 3, gen)
        s1 = Banks(ctx, nc, tag + "s1", 2, s1, 2 * BANK)
        acc = Banks(ctx, nc, tag + "acc", 1, acc)
        params = [(bqc[:], bq), (bkc[:], bk), (bvr[:], bv), (bor[:], bo)]

        block = ctx.enter_context(nc.Block())

        @block.sync
        def _(sp):
            for s in src_loaded + [mask_loaded] + rows_loaded + res_loaded + stored:
                s.start(sp)
            for n in range(3):
                if n >= 2:
                    sp.wait_ge(half_ready, n - 1)
                sp.dma_start(stage[n % 2], wts[n].rearrange("(k p) n -> p k n", p=P)).then_inc(stage_loaded[n % 2], 16)
            for t, a in params + [(wo[:], wts[3].rearrange("(k p) n -> p k n", p=P))]:
                sp.dma_start(t, a).then_inc(par_loaded, 16)
            sp.wait_ge(half_ready, 3)
            with sp.Fori(0, B) as it:
                def load_src(n):
                    sp.wait_ge(srcT_full.sem, srcT_full.at(it, n - 2))
                    sp.sem_inc(passed_sp, 1)
                    if n < 2:
                        sp.wait_ge(stored[n].sem, stored[n].at(it, -1))
                        sp.sem_inc(passed_sp, 1)
                    a, t = (ctx_in, n) if n < NT else (x_in, n - NT)
                    sp.dma_start(src[:, n % 2, :], a[it, t * P:(t + 1) * P, :]).then_inc(src_loaded[n % 2].sem, 16)

                def mask(_):
                    sp.wait_ge(mask_ready.sem, mask_ready.at(it, -1))
                    sp.sem_inc(passed_sp, 1)
                    sp.dma_start(mask8[ROW_MASK:ROW_MASK + 1, :], mask_in[bass.ds(it, 1), :])\
                        .then_inc(mask_loaded.sem, 16)

                def load(h):
                    g, a = h // HG, h % HG * XD
                    sp.wait_ge(klo_ready.sem, klo_ready.at(it, 2 * g + 1))
                    sp.sem_inc(passed_sp, 1)
                    sp.wait_ge(qlo_ready.sem, qlo_ready.at(it, 2 * g + 1))
                    sp.sem_inc(passed_sp, 1)
                    sp.wait_ge(s2_full.sem, s2_full.at(it, NP * (before(h) + 1) - 1))
                    sp.sem_inc(passed_sp, 1)
                    s = slot(h)
                    for i, (q, k) in enumerate(((q_hi, k_hi), (q_hi, k_lo), (q_lo, k_hi))):
                        sp.dma_start(qa[s][i * XD:(i + 1) * XD, :].bitcast(F32), q[a:a + XD, :].bitcast(F32))\
                           .then_inc(rows_loaded[s].sem, 16)
                        sp.dma_start(ka[s][i * XD:(i + 1) * XD, :].bitcast(F32), k[a:a + XD, g, :].bitcast(F32))\
                           .then_inc(rows_loaded[s].sem, 16)

                def output(t):
                    def load_res(t):
                        sp.wait_ge(stored[t % 2].sem, stored[t % 2].at(it, t // 2 - 1))
                        sp.sem_inc(passed_sp, 1)
                        sp.dma_start(res[:, t % 2, :], x_in[it, t * P:(t + 1) * P, :]).then_inc(res_loaded[t % 2].sem, 16)

                    if t == 0:
                        sp.wait_ge(srcT_full.sem, srcT_full.at(it, 2 * NT - 1))
                        sp.sem_inc(passed_sp, 1)
                        load_res(0)
                    if t + 1 < NT:
                        load_res(t + 1)
                    sp.wait_ge(out_ready.sem, out_ready.at(it, t))
                    sp.sem_inc(passed_sp, 1)
                    sp.dma_start(out[it, t * P:(t + 1) * P, :], res[:, t % 2, :]).then_inc(stored[t % 2].sem, 16)

                run({"src": load_src, "mask": mask, "load": load, "o": output})
            for s in stored:
                sp.wait_ge(s.sem, (B + 1) * s.per * 16)

        @block.gpsimd
        def _(pool):
            resb_ready.start(pool)
            g_ = nc.gpsimd
            for t in (later_k, later_q):
                g_.memset(t[:], 0.0)
            identity(nc, pool, const_ready, [ident[:], ident_b[:]])
            g_.affine_select(later_k[:], later_k[:], [[1, P]], ALU.is_ge, NEG, base=0, channel_multiplier=-1)
            g_.affine_select(later_q[:], later_q[:], [[-1, P]], ALU.is_ge, NEG, base=0, channel_multiplier=1)\
                .then_inc(const_ready, 1)
            pool.wait_ge(par_loaded, 16 * (len(params) + 1))
            with pool.Fori(0, B) as it:
                for t in range(NT):
                    pool.wait_ge(res_loaded[t % 2].sem, res_loaded[t % 2].at(it, t // 2))
                    g_.tensor_tensor(res[:, t % 2, :], res[:, t % 2, :], bor[:], ALU.add).then_inc(resb_ready.sem, 1)

        @block.scalar
        def _(act):
            for s in [shi_ready, khi_ready, qhi_ready, p_ready, oT_ready]:
                s.start(act)
            a_ = nc.scalar
            act.wait_ge(par_loaded, 16 * (len(params) + 1))
            with act.Fori(0, B) as it:
                def source(n):
                    act.wait_ge(srcT_full.sem, srcT_full.at(it, n))
                    if n < NT:
                        act.wait_ge(q_full.sem, q_full.at(it, -1))
                    else:
                        act.wait_ge(v_full.sem, v_full.at(it, NT - 1))
                    t = n % NT
                    a_.activation(st_hi[:, :, t * P:(t + 1) * P], gen["src", n][:].rearrange("p (k n) -> p k n", k=KD), ACT.Copy)\
                        .then_inc(shi_ready.sem, 1)

                def keys(i):
                    g, j = i // 2, i % 2
                    act.wait_ge(k_full.sem, k_full.at(it, i))
                    for s in range(SLOTS):
                        act.wait_ge(rows_loaded[s].sem, rows_loaded[s].at(it, -1))
                    a_.activation(k_hi[:, g, j * BANK:(j + 1) * BANK], gen["k", i][:], ACT.Identity, bias=bkc[:, g:g + 1])\
                        .then_inc(khi_ready.sem, 1)

                def queries(i):
                    g, j = i // 2, i % 2
                    act.wait_ge(q_full.sem, q_full.at(it, i))
                    for s in range(SLOTS):
                        n = sum(h < HG * g for h in used[s])
                        act.wait_ge(rows_loaded[s].sem, rows_loaded[s].at(it, 6 * n - 1))
                    a_.activation(q_hi[:, j * BANK:(j + 1) * BANK], gen["q", i][:], ACT.Identity, bias=bqc[:, g:g + 1])\
                        .then_inc(qhi_ready.sem, 1)

                def exps(h, s):
                    n = h * NP + s
                    act.wait_ge(s2_full.sem, s2_full.at(it, n))
                    act.wait_ge(av_full.sem, av_full.at(it, n - 4))
                    w = PC[s][2]
                    a_.activation(pe_x[:, n % 4, 0:w], gen["p2", h, s][:, 0:w], ACT.Exp, scale=XSCALE).then_inc(p_ready.sem, 1)

                def output(t):
                    act.wait_ge(oT_full.sem, oT_full.at(it, t))
                    act.wait_ge(o_full.sem, o_full.at(it, t - 1))
                    a_.activation(oT[:], gen["oT", t][:].rearrange("p (k n) -> p k n", k=KD), ACT.Copy).then_inc(oT_ready.sem, 1)

                run({"src": source, "k": keys, "q": queries, "p2": exps, "o": output})

        @block.vector
        def _(dve):
            for s in [mask_ready, xn_ready, slo_ready, klo_ready, v_ready, qlo_ready, mx_ready, nm_ready, mrow_ready,
                      rc_ready, head_ready, out_ready, dve_step]:
                s.start(dve)
            v_ = nc.vector
            for n in range(3):
                split_weight(nc, dve, stage[n % 2], stage_loaded[n % 2], hi_ready, half_ready, n, w_hi[n][:], w_lo[n][:])
            v_.memset(vv[:, :, :, XD:VW], 1.0)
            v_.memset(mrow[:], 1.0)
            for t in qa + ka:
                last = v_.memset(t[ROW_MASK:ROW_MAX + 1, :].bitcast(F32), 1.0)
            last.then_inc(const_dve, 1)
            dve.wait_ge(const_dve, 1)
            dve.wait_ge(par_loaded, 16 * (len(params) + 1))
            with dve.Fori(0, B) as it:
                step = Chain(dve_step, dve, it)

                def source(n):
                    t = n % NT
                    if n >= NT:
                        x = src[:, n % 2, :]
                        dve.wait_ge(src_loaded[n % 2].sem, src_loaded[n % 2].at(it, n // 2))
                        dve.wait_ge(xn_ready.sem, xn_ready.at(it, n - NT - 1))
                        step(v_.bn_stats(stat[:], x))
                        dve.sem_inc(passed_dve, 1)
                        step(v_.bn_aggr(mv[:], stat[:]))
                        rsqrt(nc, step, xr[:], mv[:, 1:2], tmp[:, 0:1], tmp[:, 1:2], 1.0, EPS)
                        v_.tensor_scalar(x, x, mv[:, 0:1], xr[:, 0:1], ALU.subtract, ALU.mult).then_inc(xn_ready.sem, 1)
                    dve.wait_ge(shi_ready.sem, shi_ready.at(it, n))
                    sl = slice(t * P, (t + 1) * P)
                    v_.tensor_tensor(st_lo[:, :, sl], gen["src", n][:].rearrange("p (k n) -> p k n", k=KD),
                                     st_hi[:, :, sl].bitcast(F32), ALU.subtract).then_inc(slo_ready.sem, 1)

                def mask(_):
                    dve.wait_ge(mask_loaded.sem, mask_loaded.at(it, 0))
                    dve.wait_ge(s2_full.sem, s2_full.at(it, -1))
                    for t in ka:
                        last = v_.tensor_scalar(t[ROW_MASK:ROW_MASK + 1, :], mask8[ROW_MASK:ROW_MASK + 1, :], NEG, None, ALU.mult)
                    last.then_inc(mask_ready.sem, 1)

                def keys(i):
                    g, j = i // 2, i % 2
                    sl = slice(j * BANK, (j + 1) * BANK)
                    dve.wait_ge(khi_ready.sem, khi_ready.at(it, i))
                    v_.scalar_tensor_tensor(k_lo[:, g, sl], gen["k", i][:], bkc[:, g:g + 1], k_hi[:, g, sl].bitcast(F32),
                                            ALU.add, ALU.subtract).then_inc(klo_ready.sem, 1)

                def values(t):
                    dve.wait_ge(v_full.sem, v_full.at(it, t))
                    dve.wait_ge(av_full.sem, av_full.at(it, -1))
                    v_.tensor_tensor(vv[:, t, :, 0:XD], gen["v", t][:].rearrange("p (h d) -> p h d", h=XH),
                                     bvr[:].rearrange("p (h d) -> p h d", h=XH), ALU.add).then_inc(v_ready.sem, 1)

                def queries(i):
                    g, j = i // 2, i % 2
                    sl = slice(j * BANK, (j + 1) * BANK)
                    dve.wait_ge(qhi_ready.sem, qhi_ready.at(it, i))
                    v_.scalar_tensor_tensor(q_lo[:, sl], gen["q", i][:], bqc[:, g:g + 1], q_hi[:, sl].bitcast(F32),
                                            ALU.add, ALU.subtract).then_inc(qlo_ready.sem, 1)

                def maxima(h, i):
                    n = h * NT + i
                    dve.wait_ge(s1_full.sem, s1_full.at(it, n))
                    if i == 0:
                        dve.wait_ge(nm_ready.sem, nm_ready.at(it, h - 2))
                    v_.tensor_reduce(mx[:, h % 2, i:i + 1], s1[h, i][:, 0:(i + 1) * P], AX.X, ALU.max).then_inc(mx_ready.sem, 1)

                def negate(h):
                    dve.wait_ge(mx_ready.sem, mx_ready.at(it, NT * h + NT - 1))
                    dve.wait_ge(mT_full.sem, mT_full.at(it, 2 * (h - 2) + 1))
                    v_.tensor_scalar(mrow[:, h % 2, :, 1], mx[:, h % 2, :], -1.0, None, ALU.mult).then_inc(nm_ready.sem, 1)
                    for j in range(2):
                        dve.wait_ge(mT_full.sem, mT_full.at(it, 2 * h + j))
                        v_.tensor_copy(qa[slot(h)][ROW_MASK:ROW_MAX + 1, j * BANK:(j + 1) * BANK], gen["mT", h, j][0:2, :])\
                            .then_inc(mrow_ready.sem, 1)

                def head(h):
                    a = acc[h][:, 0:NT * VW].rearrange("p (t d) -> p t d", t=NT)
                    dve.wait_ge(av_full.sem, av_full.at(it, NP * h + NP - 1))
                    dve.wait_ge(head_ready.sem, head_ready.at(it, h - 1))
                    v_.reciprocal(rc[:], a[:, :, XD]).then_inc(rc_ready.sem, 1)
                    dve.wait_ge(rc_ready.sem, rc_ready.at(it, h))
                    if h == 0:
                        dve.wait_ge(oT_full.sem, oT_full.at(it, -1))
                    v_.tensor_tensor(oo[:, :, h * XD:(h + 1) * XD], a[:, :, 0:XD], bcast(rc[:], 2, XD), ALU.mult)\
                        .then_inc(head_ready.sem, 1)

                def output(t):
                    dve.wait_ge(resb_ready.sem, resb_ready.at(it, t))
                    dve.wait_ge(o_full.sem, o_full.at(it, t))
                    v_.tensor_tensor(res[:, t % 2, :], gen["o", t][:], res[:, t % 2, :], ALU.add).then_inc(out_ready.sem, 1)

                run({"src": source, "mask": mask, "k": keys, "v": values, "q": queries, "p1": maxima, "nm": negate,
                     "head": head, "o": output})

        @block.tensor
        def _(pe):
            for s in [srcT_full, k_full, v_full, q_full, s1_full, mT_full, s2_full, av_full, oT_full, o_full]:
                s.start(pe)
            mm, tr = nc.tensor.matmul, nc.tensor.transpose
            pe.wait_ge(const_ready, 3)
            pe.wait_ge(const_dve, 1)
            pe.wait_ge(par_loaded, 16 * (len(params) + 1))
            with pe.Fori(0, B) as it:
                def source(n):
                    if n < NT:
                        pe.wait_ge(src_loaded[n % 2].sem, src_loaded[n % 2].at(it, n // 2))
                    else:
                        pe.wait_ge(xn_ready.sem, xn_ready.at(it, n - NT))
                    ps = gen.open(pe, it, ("src", n))
                    for k in range(KD):
                        last = tr(ps[:, k * P:(k + 1) * P], src[:, n % 2, k * P:(k + 1) * P], ident[:])
                    last.then_inc(srcT_full.sem, 1)

                def channels(what, w, i, full):
                    g, j = i // 2, i % 2
                    ps = gen.open(pe, it, (what, i))
                    for k in range(KD):
                        cols, sl = slice(g * P, (g + 1) * P), slice(j * BANK, (j + 1) * BANK)
                        last = matmul3(nc, ps[:], w_hi[w][:, k, cols], w_lo[w][:, k, cols], st_hi[:, k, sl], st_lo[:, k, sl],
                                       k == 0, k == KD - 1)
                    last.then_inc(full.sem, 1)

                def keys(i):
                    pe.wait_ge(slo_ready.sem, slo_ready.at(it, NT - 1))
                    channels("k", 1, i, k_full)

                def queries(i):
                    pe.wait_ge(slo_ready.sem, slo_ready.at(it, 2 * NT - 1))
                    channels("q", 0, i, q_full)

                def values(t):
                    ps = gen.open(pe, it, ("v", t))
                    sl = slice(t * P, (t + 1) * P)
                    for k in range(KD):
                        last = matmul3(nc, ps[:], st_hi[:, k, sl], st_lo[:, k, sl], w_hi[2][:, k, :], w_lo[2][:, k, :],
                                       k == 0, k == KD - 1)
                    last.then_inc(v_full.sem, 1)

                def pass1(h, i):
                    s = slot(h)
                    if i == 0:
                        pe.wait_ge(rows_loaded[s].sem, rows_loaded[s].at(it, 6 * used[s].index(h) + 5))
                        pe.wait_ge(mask_ready.sem, mask_ready.at(it, 0))
                    ps = s1.open(pe, it, (h, i))
                    n = (i + 1) * P
                    for a in range(0, n, BANK):
                        b = min(n, a + BANK)
                        mm(ps[:, a:b], qa[s][0:ROW_MAX, i * P:(i + 1) * P], ka[s][0:ROW_MAX, a:b], start=True, stop=b < n)
                    mm(ps[:, i * P:n], ident_b[:], later_q[:], start=False, stop=True).then_inc(s1_full.sem, 1)

                def rows(h):
                    pe.wait_ge(nm_ready.sem, nm_ready.at(it, h))
                    for j in range(2):
                        ps = gen.open(pe, it, ("mT", h, j))
                        for t in range(4):
                            last = tr(ps[0:2, t * P:(t + 1) * P], mrow[:, h % 2, 4 * j + t, :], ident[:])
                        last.then_inc(mT_full.sem, 1)

                def pass2(h, s):
                    j, a, n = PC[s]
                    sl = slot(h)
                    if s == 0:
                        pe.wait_ge(mrow_ready.sem, mrow_ready.at(it, 2 * h + 1))
                    ps = gen.open(pe, it, ("p2", h, s))
                    diagonal = a == j * P
                    last = mm(ps[:, 0:n], ka[sl][0:ROW_MAX + 1, j * P:(j + 1) * P], qa[sl][0:ROW_MAX + 1, a:a + n],
                              start=True, stop=not diagonal)
                    if diagonal:
                        last = mm(ps[:, 0:P], ident_b[:], later_k[:], start=False, stop=True)
                    last.then_inc(s2_full.sem, 1)

                def weigh(h, s):
                    j, a, n = PC[s]
                    pe.wait_ge(p_ready.sem, p_ready.at(it, h * NP + s))
                    if h == 0 and s == 0:
                        pe.wait_ge(v_ready.sem, v_ready.at(it, NT - 1))
                    ps = acc.open(pe, it, h) if s == 0 else acc[h]
                    for i in range(n // P):
                        t = a // P + i
                        last = mm(ps[:, t * VW:(t + 1) * VW], pe_x[:, (h * NP + s) % 4, i * P:(i + 1) * P], vv[:, j, h, :],
                                  start=s == 0 and i == 0, stop=s == NP - 1, skip_group_check=True)
                    last.then_inc(av_full.sem, 1)

                def output(t):
                    if t == 0:
                        pe.wait_ge(head_ready.sem, head_ready.at(it, XH - 1))
                    ps = gen.open(pe, it, ("oT", t))
                    for k in range(KD):
                        last = tr(ps[:, k * P:(k + 1) * P], oo[:, t, k * P:(k + 1) * P], ident[:])
                    last.then_inc(oT_full.sem, 1)
                    pe.wait_ge(oT_ready.sem, oT_ready.at(it, t))
                    ps = gen.open(pe, it, ("o", t))
                    for k in range(KD):
                        last = mm(ps[:], oT[:, k, :], wo[:, k, :], start=k == 0, stop=k == KD - 1)
                    last.then_inc(o_full.sem, 1)

                run({"src": source, "k": keys, "v": values, "q": queries, "p1": pass1, "nm": rows, "p2": pass2,
                     "av": weigh, "o": output})
    release(nc, held)


NE = 16
HD = 64
EW = 3 * NE * HD
EH = BANK // HD
KO = NE * HD // P
HW = EW // 2
STAGES = 2 * KD + KO // 2
TINY = 1e12
FVW = HD + 1


def moe_attention(nc, x_in, wqkv, w_o, sim, gates, out):
    tag = "ff_"
    PC = pieces()
    NP = len(PC)
    held = []
    with ExitStack() as ctx:
        def sb(name, shape, dt=F32):
            return ctx.enter_context(nc.sbuf_tensor(tag + name, shape, dt))

        def sig(name, per, unit=1):
            return Signal(held, nc, tag + name, per, unit)

        def sem(name):
            held.append(nc.alloc_semaphore(tag + name))
            return held[-1]

        w_hi, w_lo = sb("w_hi", [P, KD, EW], F32R), sb("w_lo", [P, KD, EW], F32R)
        wo_hi, wo_lo = sb("wo_hi", [P, KO, D], F32R), sb("wo_lo", [P, KO, D], F32R)
        ident, ident_b = sb("ident", [P, P]), sb("ident_b", [P, P], BF16)
        later_k, later_q = sb("later_k", [P, P], BF16), sb("later_q", [P, P], BF16)
        ones = sb("ones", [P, P])
        rev = sb("rev", [P, NE])
        simw, simq = sb("simw", [P, KD, NE]), sb("simq", [P, KD, NE])
        sim_hi, sim_lo = sb("sim_hi", [P, KD, NE], F32R), sb("sim_lo", [P, KD, NE], F32R)
        sgm, sg1 = sb("sgm", [P, NE]), sb("sg1", [P, NE])
        cn, cn1, cn2 = sb("cn", [P, NE]), sb("cn1", [P, NE]), sb("cn2", [P, NE])
        src = sb("src", [P, 2, D])
        squares = sb("squares", [P, D], BF16)
        stat, mv, xr, tmp2 = sb("stat", [P, 6]), sb("mv", [P, 2]), sb("xr", [P, 1]), sb("tmp2", [P, 2])
        ss, rn, rn1, rn2 = sb("ss", [P, NT]), sb("rn", [P, NT]), sb("rn1", [P, NT]), sb("rn2", [P, NT])
        st_hi, st_lo = sb("st_hi", [P, KD, S], F32R), sb("st_lo", [P, KD, S], F32R)
        lg, ga, gb_, gc, gd, ge = [sb(n, [P, NT, NE]) for n in ("lg", "ga", "gb", "gc", "gd", "ge")]
        m1, m2 = sb("m1", [P, NT]), sb("m2", [P, NT])
        rw = sb("rw", [P, NT, NE])
        work = sb("work", [P, 5 * DI])
        pe_x = work[:, 0:4 * BANK].rearrange("p (r n) -> p r n", r=4)
        mixed = work[:, 0:2 * DI].rearrange("p (r n) -> p r n", r=2)
        parts = work[:, 2 * DI:3 * DI].rearrange("p (e d) -> p e d", e=NE)
        qa, ka = work[:, 3 * DI:4 * DI], work[:, 4 * DI:5 * DI]
        stage = [work[:, i * HW:(i + 1) * HW] for i in range(2)]
        qk = sb("qk", [P, 2, 2, HD])
        vv = sb("vv", [P, NT, FVW])
        mx, mneg, rc = sb("mx", [P, NT]), sb("mneg", [P, NT]), sb("rc", [P, NT])
        at = sb("at", [P, NT, HD])
        mT_hi, mT_lo = sb("mT_hi", [P, KO, P], F32R), sb("mT_lo", [P, KO, P], F32R)

        src_loaded = [sig(f"src_loaded{i}", NT // 2, 16) for i in range(2)]
        xn_ready = sig("xn_ready", NT)
        ss_ready = sig("ss_ready", NT)
        srcT_full = sig("srcT_full", NT)
        shi_ready, slo_ready = sig("shi_ready", NT), sig("slo_ready", NT)
        lg_full = sig("lg_full", NT)
        lg_ready = sig("lg_ready", 1)
        arg_ready = sig("arg_ready", 1)
        ex_ready = sig("ex_ready", 1)
        rw_ready = sig("rw_ready", 1)
        w_full = sig("w_full", NT * 6)
        part_ready = sig("part_ready", NT * 6)
        qkv_ready = sig("qkv_ready", NT * 3)
        qkT_full = sig("qkT_full", NT)
        qkT_ready = sig("qkT_ready", NT)
        s1_full, mx_ready = sig("s1_full", NT), sig("mx_ready", NT)
        nm_ready = sig("nm_ready", 1)
        mT_full, mrow_ready = sig("mT_full", 2), sig("mrow_ready", 2)
        s2_full, p_ready, av_full = sig("s2_full", NP), sig("p_ready", NP), sig("av_full", NP)
        rc_ready = sig("rc_ready", 1)
        at_ready = sig("at_ready", 1)
        mixed_ready = sig("mixed_ready", NT)
        mixT_full = sig("mixT_full", NT * 2)
        mhi_ready, mlo_ready = sig("mhi_ready", NT * 2), sig("mlo_ready", NT * 2)
        o_full = sig("o_full", NT)
        res_loaded = [sig(f"res_loaded{i}", NT // 2, 16) for i in range(2)]
        out_ready = sig("out_ready", NT)
        stored = [sig(f"stored{i}", NT // 2, 16) for i in range(2)]
        GATE = 16
        steps = NT * (2 + RSQRT_STEPS) + RSQRT_STEPS + 1 + GATE + 5
        dve_step = sig("dve_step", steps)
        const_ready, par_loaded, const_dve = sem("const_ready"), sem("par_loaded"), sem("const_dve")
        stage_loaded = [sem(f"stage_loaded{i}") for i in range(2)]
        hi_ready, half_ready = sem("hi_ready"), sem("half_ready")
        sg_ready, sim_full, sim_step = sem("sg_ready"), sem("sim_full"), sig("sim_step", 1)
        passed_sp, passed_dve = sem("passed_sp"), sem("passed_dve")

        def order():
            for t in range(NT):
                yield "src", t
            yield "gate", 0
            for t in range(NT):
                yield "qkv", t
                if t:
                    yield "qkT", t - 1
                    yield "p1", t - 1
            yield "qkT", NT - 1
            yield "p1", NT - 1
            yield "nm", 0
            for s in range(NP):
                yield "p2", s
                if s >= 2:
                    yield "av", s - 2
            yield "av", NP - 2
            yield "av", NP - 1
            yield "at", 0
            for t in range(NT):
                yield "mix", t
                if t:
                    yield "o", t - 1
            yield "o", NT - 1

        def run(steps):
            for what, n in order():
                if what in steps:
                    steps[what](n)

        gen, s1, acc = [], [], []
        for what, n in order():
            if what == "src":
                gen += [(("src", n), slo_ready, n)]
            if what == "qkv":
                gen += [(("w", n, c), part_ready, 6 * n + c) for c in range(6)]
            if what == "qkT":
                gen += [(("qkT", n), qkT_ready, n)]
            if what == "p1":
                s1 += [(n, mx_ready, n)]
            if what == "nm":
                gen += [(("mT", j), mrow_ready, j) for j in range(2)]
            if what == "p2":
                gen += [(("p2", n), p_ready, n)]
            if what == "at":
                acc += [(j, at_ready, 0) for j in range(2)]
            if what == "mix":
                gen += [(("mT8", n, j), mlo_ready, 2 * n + j) for j in range(2)]
            if what == "o":
                gen += [(("o", n), out_ready, n)]
        s1_uses = s1
        gen = Banks(ctx, nc, tag + "gen", 3, gen)
        s1 = Banks(ctx, nc, tag + "s1", 1, s1_uses, 2 * BANK)
        acc = Banks(ctx, nc, tag + "acc", 2, acc)
        lgb = Banks(ctx, nc, tag + "lg", 1, [(0, lg_ready, 0)])

        block = ctx.enter_context(nc.Block())

        @block.sync
        def _(sp):
            for s in src_loaded + res_loaded + stored:
                s.start(sp)
            for n in range(STAGES):
                if n >= 2:
                    sp.wait_ge(half_ready, n - 1)
                if n < 2 * KD:
                    k, cols = n // 2, slice(n % 2 * HW, (n % 2 + 1) * HW)
                    sp.dma_start(stage[n % 2], wqkv[k * P:(k + 1) * P, cols]).then_inc(stage_loaded[n % 2], 16)
                else:
                    k = 2 * (n - 2 * KD)
                    sp.dma_start(stage[n % 2][:, 0:2 * D].rearrange("p (k n) -> p k n", k=2),
                                 w_o[k * P:(k + 2) * P, :].rearrange("(k p) n -> p k n", p=P)).then_inc(stage_loaded[n % 2], 16)
                if n == 0:
                    sp.dma_start(simw[:], sim.rearrange("(k p) n -> p k n", p=P)).then_inc(par_loaded, 16)
                    sp.dma_start(sgm[:], gates).then_inc(par_loaded, 16)
            with sp.Fori(0, B) as it:
                def load_src(t):
                    sp.wait_ge(srcT_full.sem, srcT_full.at(it, t - 2))
                    sp.sem_inc(passed_sp, 1)
                    sp.wait_ge(ss_ready.sem, ss_ready.at(it, t - 2))
                    sp.sem_inc(passed_sp, 1)
                    if t < 2:
                        sp.wait_ge(stored[t].sem, stored[t].at(it, -1))
                        sp.sem_inc(passed_sp, 1)
                    sp.dma_start(src[:, t % 2, :], x_in[it, t * P:(t + 1) * P, :]).then_inc(src_loaded[t % 2].sem, 16)

                def load_res(t):
                    sp.wait_ge(stored[t % 2].sem, stored[t % 2].at(it, t // 2 - 1))
                    sp.sem_inc(passed_sp, 1)
                    sp.dma_start(src[:, t % 2, :], x_in[it, t * P:(t + 1) * P, :]).then_inc(res_loaded[t % 2].sem, 16)

                def output(t):
                    if t == 0:
                        for s in (srcT_full, ss_ready):
                            sp.wait_ge(s.sem, s.at(it, NT - 1))
                            sp.sem_inc(passed_sp, 1)
                        load_res(0)
                    if t + 1 < NT:
                        load_res(t + 1)
                    sp.wait_ge(out_ready.sem, out_ready.at(it, t))
                    sp.sem_inc(passed_sp, 1)
                    sp.dma_start(out[it, t * P:(t + 1) * P, :], src[:, t % 2, :]).then_inc(stored[t % 2].sem, 16)

                run({"src": load_src, "o": output})
            for s in stored:
                sp.wait_ge(s.sem, (B + 1) * s.per * 16)

        @block.gpsimd
        def _(pool):
            mixed_ready.start(pool)
            g_ = nc.gpsimd
            g_.memset(ones[:], 1.0)
            for t in (later_k, later_q):
                g_.memset(t[:], 0.0)
            identity(nc, pool, const_ready, [ident[:], ident_b[:]])
            g_.affine_select(later_k[:], later_k[:], [[1, P]], ALU.is_ge, NEG, base=0, channel_multiplier=-1)
            g_.affine_select(later_q[:], later_q[:], [[-1, P]], ALU.is_ge, NEG, base=0, channel_multiplier=1)
            for e in range(NE):
                last = g_.memset(rev[:, e:e + 1], float(NE - e))
            last.then_inc(const_ready, 1)
            pool.wait_ge(half_ready, STAGES)
            with pool.Fori(0, B) as it:
                for t in range(NT):
                    if t == 0:
                        pool.wait_ge(at_ready.sem, at_ready.at(it, 0))
                    pool.wait_ge(mixT_full.sem, mixT_full.at(it, 2 * (t - 2) + 1))
                    g_.tensor_tensor(mixed[:, t % 2, :].rearrange("p (e d) -> p e d", e=NE), bcast(at[:, t, :], 1, NE),
                                     bcast(rw[:, t, :], 2, HD), ALU.mult).then_inc(mixed_ready.sem, 1)

        @block.scalar
        def _(act):
            for s in [ss_ready, shi_ready, ex_ready, qkT_ready, p_ready, mhi_ready]:
                s.start(act)
            a_ = nc.scalar
            act.wait_ge(par_loaded, 32)
            a_.activation(sg1[:], sgm[:], ACT.Exp, scale=-1.0).then_inc(sg_ready, 1)
            act.wait_ge(half_ready, STAGES)
            with act.Fori(0, B) as it:
                def source(t):
                    act.wait_ge(xn_ready.sem, xn_ready.at(it, t))
                    act.wait_ge(rw_ready.sem, rw_ready.at(it, -1))
                    a_.activation(squares[:], src[:, t % 2, :], ACT.Square, accum_out=ss[:, t:t + 1]).then_inc(ss_ready.sem, 1)
                    act.wait_ge(srcT_full.sem, srcT_full.at(it, t))
                    act.wait_ge(w_full.sem, w_full.at(it, -1))
                    a_.activation(st_hi[:, :, t * P:(t + 1) * P], gen["src", t][:].rearrange("p (k n) -> p k n", k=KD), ACT.Copy)\
                        .then_inc(shi_ready.sem, 1)

                def gate(_):
                    act.wait_ge(arg_ready.sem, arg_ready.at(it, 0))
                    a_.activation(gc[:], gb_[:], ACT.Exp).then_inc(ex_ready.sem, 1)

                def rows(t):
                    act.wait_ge(qkT_full.sem, qkT_full.at(it, t))
                    act.wait_ge(s2_full.sem, s2_full.at(it, -1))
                    sl = slice(t * P, (t + 1) * P)
                    a_.activation(qa[0:HD, sl], gen["qkT", t][0:HD, 0:P], ACT.Copy)
                    a_.activation(ka[0:HD, sl], gen["qkT", t][HD:P, 0:P], ACT.Copy).then_inc(qkT_ready.sem, 1)

                def exps(s):
                    n = PC[s][2]
                    act.wait_ge(s2_full.sem, s2_full.at(it, s))
                    act.wait_ge(av_full.sem, av_full.at(it, s - 4))
                    a_.activation(pe_x[:, s % 4, 0:n], gen["p2", s][:, 0:n], ACT.Exp, scale=HD ** -0.5).then_inc(p_ready.sem, 1)

                def mix(t):
                    act.wait_ge(o_full.sem, o_full.at(it, t - 1))
                    for j in range(2):
                        act.wait_ge(mixT_full.sem, mixT_full.at(it, 2 * t + j))
                        a_.activation(mT_hi[:, 4 * j:4 * j + 4, :], gen["mT8", t, j][:].rearrange("p (k n) -> p k n", k=4),
                                      ACT.Copy).then_inc(mhi_ready.sem, 1)

                run({"src": source, "gate": gate, "qkT": rows, "p2": exps, "mix": mix})

        @block.vector
        def _(dve):
            for s in [xn_ready, slo_ready, lg_ready, arg_ready, rw_ready, part_ready, qkv_ready, mx_ready, nm_ready,
                      mrow_ready, rc_ready, at_ready, mlo_ready, out_ready, dve_step]:
                s.start(dve)
            v_ = nc.vector
            for n in range(STAGES):
                if n < 2 * KD:
                    k, cols = n // 2, slice(n % 2 * HW, (n % 2 + 1) * HW)
                    split_weight(nc, dve, stage[n % 2], stage_loaded[n % 2], hi_ready, half_ready, n, w_hi[:, k, cols], w_lo[:, k, cols])
                else:
                    k = 2 * (n - 2 * KD)
                    split_weight(nc, dve, stage[n % 2][:, 0:2 * D].rearrange("p (k n) -> p k n", k=2), stage_loaded[n % 2],
                                 hi_ready, half_ready, n, wo_hi[:, k:k + 2, :], wo_lo[:, k:k + 2, :])
            step = Chain(sim_step, dve, 0)
            sim_step.start(dve)
            dve.wait_ge(par_loaded, 32)
            step(v_.tensor_tensor(simq[:], simw[:], simw[:], ALU.mult))
            dve.wait_ge(sim_full, 1)
            rsqrt(nc, step, cn[:], gen.t[0][:, 0:NE], cn1[:], cn2[:], 1.0, 0.0)
            step(v_.tensor_scalar(cn[:], cn[:], TINY, None, ALU.min))
            step(v_.tensor_tensor(simw[:], simw[:], bcast(cn[:], 1, KD), ALU.mult))
            step(v_.tensor_copy(sim_hi[:], simw[:]))
            step(v_.tensor_tensor(sim_lo[:], simw[:], sim_hi[:].bitcast(F32), ALU.subtract))
            dve.wait_ge(sg_ready, 1)
            step(v_.tensor_scalar(sg1[:], sg1[:], 1.0, None, ALU.add))
            step(v_.reciprocal(sgm[:], sg1[:]))
            v_.memset(vv[:, :, HD:FVW], 1.0)
            v_.memset(ka[HD:HD + 1, :], 1.0).then_inc(const_dve, 1)
            dve.wait_ge(const_ready, 3)
            dve.wait_ge(const_dve, 1)
            with dve.Fori(0, B) as it:
                step = Chain(dve_step, dve, it)

                def source(t):
                    x = src[:, t % 2, :]
                    dve.wait_ge(src_loaded[t % 2].sem, src_loaded[t % 2].at(it, t // 2))
                    dve.wait_ge(xn_ready.sem, xn_ready.at(it, t - 1))
                    step(v_.bn_stats(stat[:], x))
                    dve.sem_inc(passed_dve, 1)
                    step(v_.bn_aggr(mv[:], stat[:]))
                    rsqrt(nc, step, xr[:], mv[:, 1:2], tmp2[:, 0:1], tmp2[:, 1:2], 1.0, EPS)
                    v_.tensor_scalar(x, x, mv[:, 0:1], xr[:, 0:1], ALU.subtract, ALU.mult).then_inc(xn_ready.sem, 1)
                    dve.wait_ge(shi_ready.sem, shi_ready.at(it, t))
                    sl = slice(t * P, (t + 1) * P)
                    v_.tensor_tensor(st_lo[:, :, sl], gen["src", t][:].rearrange("p (k n) -> p k n", k=KD),
                                     st_hi[:, :, sl].bitcast(F32), ALU.subtract).then_inc(slo_ready.sem, 1)

                def gate(_):
                    def wide(a):
                        return bcast(a[:], 2, NE)

                    dve.wait_ge(ss_ready.sem, ss_ready.at(it, NT - 1))
                    rsqrt(nc, step, rn[:], ss[:], rn1[:], rn2[:], 1.0, 0.0)
                    step(v_.tensor_scalar(rn[:], rn[:], TINY, None, ALU.min))
                    dve.wait_ge(lg_full.sem, lg_full.at(it, NT - 1))
                    v_.tensor_tensor(ga[:], lgb[0][:, 0:NT * NE].rearrange("p (t e) -> p t e", t=NT), wide(rn), ALU.mult)\
                        .then_inc(lg_ready.sem, 1)
                    dve.wait_ge(lg_ready.sem, lg_ready.at(it, 0))
                    step(v_.tensor_tensor(lg[:], ga[:], bcast(sgm[:], 1, NT), ALU.subtract))
                    step(v_.tensor_reduce(m1[:], lg[:], AX.X, ALU.max))
                    step(v_.tensor_tensor(ga[:], lg[:], wide(m1), ALU.is_equal))
                    step(v_.tensor_tensor(ga[:], ga[:], bcast(rev[:], 1, NT), ALU.mult))
                    step(v_.tensor_reduce(m2[:], ga[:], AX.X, ALU.max))
                    step(v_.tensor_tensor(gd[:], ga[:], wide(m2), ALU.is_equal))
                    step(v_.scalar_tensor_tensor(ge[:], gd[:], NEG, lg[:], ALU.mult, ALU.add))
                    step(v_.tensor_reduce(m2[:], ge[:], AX.X, ALU.max))
                    step(v_.tensor_tensor(ga[:], ge[:], wide(m2), ALU.is_equal))
                    step(v_.tensor_tensor(ga[:], ga[:], bcast(rev[:], 1, NT), ALU.mult))
                    step(v_.tensor_reduce(m2[:], ga[:], AX.X, ALU.max))
                    step(v_.tensor_tensor(ge[:], ga[:], wide(m2), ALU.is_equal))
                    step(v_.tensor_tensor(gd[:], gd[:], ge[:], ALU.add))
                    step(v_.tensor_scalar(m2[:], m1[:], 0.0, None, ALU.max))
                    step(v_.tensor_scalar(ga[:], lg[:], 0.0, None, ALU.max))
                    v_.tensor_tensor(gb_[:], ga[:], wide(m2), ALU.subtract).then_inc(arg_ready.sem, 1)
                    v_.tensor_scalar(m1[:], m1[:], 0.0, None, ALU.is_le)
                    step(v_.tensor_scalar(ge[:], lg[:], 0.0, None, ALU.is_gt))
                    dve.wait_ge(arg_ready.sem, arg_ready.at(it, 0))
                    step(v_.tensor_tensor(gd[:], gd[:], wide(m1), ALU.mult))
                    step(v_.tensor_tensor(gd[:], gd[:], ge[:], ALU.add))
                    dve.wait_ge(ex_ready.sem, ex_ready.at(it, 0))
                    step(v_.tensor_tensor(gc[:], gc[:], gd[:], ALU.mult))
                    step(v_.tensor_reduce(m1[:], gc[:], AX.X, ALU.add))
                    step(v_.reciprocal(m2[:], m1[:]))
                    dve.wait_ge(mixed_ready.sem, mixed_ready.at(it, -1))
                    v_.tensor_tensor(rw[:], gc[:], wide(m2), ALU.mult).then_inc(rw_ready.sem, 1)

                def qkv(t):
                    if t == 0:
                        dve.wait_ge(rw_ready.sem, rw_ready.at(it, 0))
                    if t == 0:
                        dve.wait_ge(av_full.sem, av_full.at(it, -1))
                    for i in range(3):
                        for j in range(2):
                            c = 2 * i + j
                            dve.wait_ge(w_full.sem, w_full.at(it, 6 * t + c))
                            if j == 0:
                                dve.wait_ge(qkv_ready.sem, qkv_ready.at(it, 3 * t + i - 1))
                            v_.tensor_tensor(parts[:, j * EH:(j + 1) * EH, :], gen["w", t, c][:].rearrange("p (e d) -> p e d", e=EH),
                                             bcast(rw[:, t, j * EH:(j + 1) * EH], 2, HD), ALU.mult).then_inc(part_ready.sem, 1)
                        dve.wait_ge(part_ready.sem, part_ready.at(it, 6 * t + 2 * i + 1))
                        if i == 0:
                            dve.wait_ge(qkT_full.sem, qkT_full.at(it, t - 2))
                        dst = qk[:, t % 2, i, :] if i < 2 else vv[:, t, 0:HD]
                        v_.tensor_reduce(dst, parts.rearrange("p e d -> p d e"), AX.X, ALU.add).then_inc(qkv_ready.sem, 1)

                def maxima(i):
                    dve.wait_ge(s1_full.sem, s1_full.at(it, i))
                    if i == 0:
                        dve.wait_ge(nm_ready.sem, nm_ready.at(it, -1))
                    v_.tensor_reduce(mx[:, i:i + 1], s1[i][:, 0:(i + 1) * P], AX.X, ALU.max).then_inc(mx_ready.sem, 1)

                def negate(_):
                    dve.wait_ge(mx_ready.sem, mx_ready.at(it, NT - 1))
                    v_.tensor_scalar(mneg[:], mx[:], -1.0, None, ALU.mult).then_inc(nm_ready.sem, 1)
                    for j in range(2):
                        dve.wait_ge(mT_full.sem, mT_full.at(it, j))
                        v_.tensor_copy(qa[HD:HD + 1, j * BANK:(j + 1) * BANK], gen["mT", j][0:1, :]).then_inc(mrow_ready.sem, 1)

                def attended(_):
                    dve.wait_ge(av_full.sem, av_full.at(it, NP - 1))
                    dve.wait_ge(mixed_ready.sem, mixed_ready.at(it, -1))

                    def view(j):
                        return acc[j][:, 0:4 * FVW].rearrange("p (t d) -> p t d", t=4)

                    for j in range(2):
                        last = v_.reciprocal(rc[:, 4 * j:4 * j + 4], view(j)[:, :, HD])
                    last.then_inc(rc_ready.sem, 1)
                    dve.wait_ge(rc_ready.sem, rc_ready.at(it, 0))
                    for j in range(2):
                        last = v_.tensor_tensor(at[:, 4 * j:4 * j + 4, :], view(j)[:, :, 0:HD],
                                                bcast(rc[:, 4 * j:4 * j + 4], 2, HD), ALU.mult)
                    last.then_inc(at_ready.sem, 1)

                def mix(t):
                    for j in range(2):
                        dve.wait_ge(mhi_ready.sem, mhi_ready.at(it, 2 * t + j))
                        v_.tensor_tensor(mT_lo[:, 4 * j:4 * j + 4, :], gen["mT8", t, j][:].rearrange("p (k n) -> p k n", k=4),
                                         mT_hi[:, 4 * j:4 * j + 4, :].bitcast(F32), ALU.subtract).then_inc(mlo_ready.sem, 1)

                def output(t):
                    dve.wait_ge(res_loaded[t % 2].sem, res_loaded[t % 2].at(it, t // 2))
                    dve.wait_ge(o_full.sem, o_full.at(it, t))
                    v_.tensor_tensor(src[:, t % 2, :], gen["o", t][:], src[:, t % 2, :], ALU.add).then_inc(out_ready.sem, 1)

                run({"src": source, "gate": gate, "qkv": qkv, "p1": maxima, "nm": negate, "at": attended, "mix": mix,
                     "o": output})
                assert step.n == steps, (step.n, steps)

        @block.tensor
        def _(pe):
            for s in [srcT_full, lg_full, w_full, qkT_full, s1_full, mT_full, s2_full, av_full, mixT_full, o_full]:
                s.start(pe)
            mm, tr = nc.tensor.matmul, nc.tensor.transpose
            pe.wait_ge(const_ready, 3)
            pe.wait_ge(sim_step.sem, 2)
            for k in range(KD):
                last = mm(gen.t[0][:, 0:NE], ones[:], simq[:, k, :], start=k == 0, stop=k == KD - 1)
            last.then_inc(sim_full, 1)
            pe.wait_ge(const_dve, 1)
            with pe.Fori(0, B) as it:
                def source(t):
                    pe.wait_ge(xn_ready.sem, xn_ready.at(it, t))
                    ps = gen.open(pe, it, ("src", t))
                    for k in range(KD):
                        last = tr(ps[:, k * P:(k + 1) * P], src[:, t % 2, k * P:(k + 1) * P], ident[:])
                    last.then_inc(srcT_full.sem, 1)
                    for u in ([t - 1] if t else []) + ([t] if t == NT - 1 else []):
                        logits(u)

                def logits(t):
                    sl = slice(t * P, (t + 1) * P)
                    pe.wait_ge(slo_ready.sem, slo_ready.at(it, t))
                    ps = lgb.open(pe, it, 0) if t == 0 else lgb[0]
                    for k in range(KD):
                        last = matmul3(nc, ps[:, t * NE:(t + 1) * NE], st_hi[:, k, sl], st_lo[:, k, sl],
                                       sim_hi[:, k, :], sim_lo[:, k, :], k == 0, k == KD - 1)
                    last.then_inc(lg_full.sem, 1)

                def qkv(t):
                    sl = slice(t * P, (t + 1) * P)
                    for c in range(6):
                        ps = gen.open(pe, it, ("w", t, c))
                        cols = slice(c * BANK, (c + 1) * BANK)
                        for k in range(KD):
                            last = matmul3(nc, ps[:], st_hi[:, k, sl], st_lo[:, k, sl], w_hi[:, k, cols], w_lo[:, k, cols],
                                           k == 0, k == KD - 1)
                        last.then_inc(w_full.sem, 1)

                def rows(t):
                    pe.wait_ge(qkv_ready.sem, qkv_ready.at(it, 3 * t + 1))
                    ps = gen.open(pe, it, ("qkT", t))
                    tr(ps[:, 0:P], qk[:, t % 2, :, :].rearrange("p i d -> p (i d)"), ident[:]).then_inc(qkT_full.sem, 1)

                def pass1(i):
                    pe.wait_ge(qkT_ready.sem, qkT_ready.at(it, i))
                    ps = s1.open(pe, it, i)
                    n = (i + 1) * P
                    for a in range(0, n, BANK):
                        b = min(n, a + BANK)
                        mm(ps[:, a:b], qa[0:HD, i * P:(i + 1) * P], ka[0:HD, a:b], start=True, stop=b < n)
                    mm(ps[:, i * P:n], ident_b[:], later_q[:], start=False, stop=True).then_inc(s1_full.sem, 1)

                def maxrow(_):
                    pe.wait_ge(nm_ready.sem, nm_ready.at(it, 0))
                    for j in range(2):
                        ps = gen.open(pe, it, ("mT", j))
                        for t in range(4):
                            last = tr(ps[0:1, t * P:(t + 1) * P], mneg[:, 4 * j + t:4 * j + t + 1], ident[:])
                        last.then_inc(mT_full.sem, 1)

                def pass2(s):
                    j, a, n = PC[s]
                    if s == 0:
                        pe.wait_ge(mrow_ready.sem, mrow_ready.at(it, 1))
                    ps = gen.open(pe, it, ("p2", s))
                    diagonal = a == j * P
                    last = mm(ps[:, 0:n], ka[0:HD + 1, j * P:(j + 1) * P], qa[0:HD + 1, a:a + n], start=True, stop=not diagonal)
                    if diagonal:
                        last = mm(ps[:, 0:P], ident_b[:], later_k[:], start=False, stop=True)
                    last.then_inc(s2_full.sem, 1)

                def weigh(s):
                    j, a, n = PC[s]
                    pe.wait_ge(p_ready.sem, p_ready.at(it, s))
                    if s == 0:
                        pe.wait_ge(qkv_ready.sem, qkv_ready.at(it, 3 * NT - 1))
                    if s < 2:
                        acc.open(pe, it, s)
                    for i in range(n // P):
                        t = a // P + i
                        last = mm(acc[t // 4][:, t % 4 * FVW:(t % 4 + 1) * FVW], pe_x[:, s % 4, i * P:(i + 1) * P], vv[:, j, :],
                                  start=s < 2 and i == 0, stop=s == NP - 1, skip_group_check=True)
                    last.then_inc(av_full.sem, 1)

                def mix(t):
                    pe.wait_ge(mixed_ready.sem, mixed_ready.at(it, t))
                    for j in range(2):
                        ps = gen.open(pe, it, ("mT8", t, j))
                        for k in range(4):
                            n = 4 * j + k
                            last = tr(ps[:, k * P:(k + 1) * P], mixed[:, t % 2, n * P:(n + 1) * P], ident[:])
                        last.then_inc(mixT_full.sem, 1)

                def output(t):
                    pe.wait_ge(mlo_ready.sem, mlo_ready.at(it, 2 * t + 1))
                    ps = gen.open(pe, it, ("o", t))
                    for k in range(KO):
                        last = matmul3(nc, ps[:], mT_hi[:, k, :], mT_lo[:, k, :], wo_hi[:, k, :], wo_lo[:, k, :],
                                       k == 0, k == KO - 1)
                    last.then_inc(o_full.sem, 1)

                run({"src": source, "qkv": qkv, "qkT": rows, "p1": pass1, "nm": maxrow, "p2": pass2, "av": weigh,
                     "mix": mix, "o": output})
    release(nc, held)


def decoder_layer(nc, x, ctx, mask, mamba_f, mamba_b, proj_b, ln_w, ln_b, attn_w, attn_b, ffn, out):
    part = nc.dram_tensor("part_dram", (B, S, D), F32).ap()
    after_mamba = nc.dram_tensor("after_mamba_dram", (B, S, D), F32).ap()
    after_attn = nc.dram_tensor("after_attn_dram", (B, S, D), F32).ap()
    mamba_pass(nc, False, x, *mamba_f, part)
    mamba_pass(nc, True, x, *mamba_b, part, after_mamba, proj_b, ln_w, ln_b)
    cross_attention(nc, after_mamba, ctx, mask, attn_w, *attn_b, after_attn)
    moe_attention(nc, after_attn, *ffn, out)


def layouts(i):
    import numpy as np

    def rows(a):
        return np.broadcast_to(a[None], (P,) + a.shape)

    def cols(a):
        return a.reshape(-1, P).T

    def mamba(d):
        g = {n: i[f"L0_attn_{d}_{n}"] for n in ("in_proj_w", "conv_w", "conv_b", "dt_bias", "A_log", "D", "rms_w", "out_proj_w")}
        proj = i["L0_attn_proj_w"]
        return [g["in_proj_w"].T, g["conv_w"][:, 0, :].T.reshape(MT, P, TAPS).transpose(1, 0, 2), cols(g["conv_b"]),
                rows(g["dt_bias"]), rows(g["A_log"]), rows(g["D"]), cols(g["rms_w"]), g["out_proj_w"],
                (proj[:, :D] if d == "f" else proj[:, D:]).T]

    qkv = [i[f"L0_ffn_{n}_proj"].transpose(1, 0, 2).reshape(D, NE * HD) for n in "qkv"]
    return {
        "x": i["x"], "ctx": i["ctx_1024"], "mask": i["mask_BxS2_bf0"],
        "mamba_f": mamba("f"), "mamba_b": mamba("b"),
        "proj_b": rows(i["L0_attn_proj_b"]), "ln_w": rows(i["L0_attn_ln_w"]), "ln_b": rows(i["L0_attn_ln_b"]),
        "attn_w": [i[f"L0_xattn_W_{n}"].T for n in "qkvo"],
        "attn_b": [cols(i["L0_xattn_b_q"]), cols(i["L0_xattn_b_k"]), rows(i["L0_xattn_b_v"]), rows(i["L0_xattn_b_o"])],
        "ffn": [np.concatenate(qkv, axis=1), i["L0_ffn_o_proj"].reshape(NE * HD, D), i["L0_ffn_sim_matrix"],
                rows(i["L0_ffn_gates"])],
    }


def kernel(**inputs):
    import numpy as _np
    import concourse.bacc as _bacc
    from concourse import mybir as _mybir
    from concourse.bass_utils import run_bass_kernel_spmd as _run

    nc = _bacc.Bacc("TRN2", target_bir_lowering=False, num_devices=1)
    arrays = {}

    def arg(name, a):
        a = _np.ascontiguousarray(a)
        arrays[f"in_{name}_dram"] = a
        return nc.dram_tensor(f"in_{name}_dram", a.shape, _mybir.dt.from_np(a.dtype), kind="ExternalInput").ap()

    args = {}
    for name, a in layouts({n: _np.asarray(v) for n, v in inputs.items()}).items():
        args[name] = [arg(f"{name}{n}", v) for n, v in enumerate(a)] if isinstance(a, list) else arg(name, a)
    out = nc.dram_tensor("out_dram", (B, S, D), _mybir.dt.float32, kind="ExternalOutput").ap()
    decoder_layer(nc, out=out, **args)
    r = _run(nc, [arrays], core_ids=[0])
    return r.results[0]["out_dram"]
```
